# Optimizing a Trainium2 kernel written in Bass

```python
import numpy as np
import jax
import jax.numpy as jnp

def _softmax(x, axis=-1):
    return jax.nn.softmax(x, axis=axis)

def _gelu(x):
    return jax.nn.gelu(x, approximate=True)

def _silu(x):
    return jax.nn.silu(x)

def _sigmoid(x):
    return jax.nn.sigmoid(x)

def _layernorm(x, axis=-1, eps=1e-05):
    m = jnp.mean(x, axis=axis, keepdims=True)
    v = jnp.var(x, axis=axis, keepdims=True)
    return (x - m) / jnp.sqrt(v + eps)

def _scatter_add(tgt, idx, src, axis=0):
    return tgt.at[idx].add(src)

def _segment_sum(src, seg, n):
    return jax.ops.segment_sum(src, seg, n)
kernel_name = 'mk_prb_d1_jaxref_r8_2c863d'

def setup_inputs(seed: int=0):
    np.random.seed(seed)
    _w = jnp.asarray

    def _L0_attn_setup():
        import jax, jax.numpy as jnp
        import numpy as np
        B, S, HID = (1, 128, 256)
        H, DQK, DV = (16, 128, 128)
        K = 4
        SCALE = DQK ** (-0.5)

        def _dwconv_causal(x_btc, wk, bk, seq):
            y = jax.lax.conv_general_dilated(x_btc.transpose(0, 2, 1), wk, (1,), [(K - 1, K - 1)], dimension_numbers=('NCH', 'OIH', 'NCH'), feature_group_count=wk.shape[0])
            return (y[:, :, :seq] + bk[None, :, None]).transpose(0, 2, 1)

        def _kda_forward(x, Wq, Wk, Wv, Wa, ba, Wb, bb, Wg, Wo, qc_w, qc_b, kc_w, kc_b, vc_w, vc_b, ln_g, ln_b):
            Bb, Ss, _ = x.shape
            q = x @ Wq.T
            k = x @ Wk.T
            v = x @ Wv.T
            q = jax.nn.silu(_dwconv_causal(q, qc_w, qc_b, Ss))
            k = jax.nn.silu(_dwconv_causal(k, kc_w, kc_b, Ss))
            v = jax.nn.silu(_dwconv_causal(v, vc_w, vc_b, Ss))
            q = q.reshape(Bb, Ss, H, DQK)
            k = k.reshape(Bb, Ss, H, DQK) * SCALE
            v = v.reshape(Bb, Ss, H, DV)
            a = jax.nn.sigmoid(x @ Wa.T + ba).reshape(Bb, Ss, H, DV)
            beta = jax.nn.sigmoid(x @ Wb.T + bb)

            def step(St, inp):
                kt, qt, vt, at, bt = inp
                Sk = jnp.einsum('bhij,bhj->bhi', St, kt)
                err = Sk - vt
                Sn = at[..., None] * St - (bt[..., None] * err)[..., None] * kt[:, :, None, :]
                ot = jnp.einsum('bhij,bhj->bhi', Sn, qt)
                return (Sn, ot)
            tfirst = lambda u: u.transpose(1, 0, 2, 3)
            S0 = jnp.zeros((Bb, H, DV, DQK), x.dtype)
            _, outs = jax.lax.scan(step, S0, (tfirst(k), tfirst(q), tfirst(v), tfirst(a), beta.transpose(1, 0, 2)))
            out = outs.transpose(1, 0, 2, 3)
            mu = out.mean(-1, keepdims=True)
            var = out.var(-1, keepdims=True)
            o = (out - mu) * jax.lax.rsqrt(var + 1e-05) * ln_g + ln_b
            g = jax.nn.sigmoid(x @ Wg.T).reshape(Bb, Ss, H, DV)
            o = (o * g).reshape(Bb, Ss, H * DV)
            return o @ Wo.T
        key = jax.random.key(seed)
        ks = jax.random.split(key, 12)
        w = lambda i, shape, sc=0.02: jax.random.normal(ks[i], shape, jnp.float32) * sc
        return dict(x=jax.random.normal(ks[0], (B, S, HID), jnp.float32), Wq=w(1, (H * DQK, HID)), Wk=w(2, (H * DQK, HID)), Wv=w(3, (H * DV, HID)), Wa=w(4, (H * DV, HID)), ba=jnp.zeros((H * DV,), jnp.float32), Wb=w(5, (H, HID)), bb=jnp.zeros((H,), jnp.float32), Wg=w(6, (H * DV, HID)), Wo=w(7, (HID, H * DV)), qc_w=w(8, (H * DQK, 1, K), 0.2), qc_b=jnp.zeros((H * DQK,), jnp.float32), kc_w=w(9, (H * DQK, 1, K), 0.2), kc_b=jnp.zeros((H * DQK,), jnp.float32), vc_w=w(10, (H * DV, 1, K), 0.2), vc_b=jnp.zeros((H * DV,), jnp.float32), ln_g=jnp.ones((DV,), jnp.float32), ln_b=jnp.zeros((DV,), jnp.float32))
    _L0_attn_in = _L0_attn_setup()

    def _L0_ffn_setup():
        import jax, jax.numpy as jnp
        import numpy as np
        E, K = (16, 4)
        C, H = (256, 448)
        B, T = (2, 64)
        STD = 0.02
        key = jax.random.key(seed)
        ks = jax.random.split(key, 5)
        x = jax.random.normal(ks[0], (B, T, C), jnp.float32)
        W_up = jax.random.normal(ks[1], (E, H, C), jnp.float32) * STD
        W_gate = jax.random.normal(ks[2], (E, H, C), jnp.float32) * STD
        W_down = jax.random.normal(ks[3], (E, C, H), jnp.float32) * STD
        gate_inp = jax.random.normal(ks[4], (E, C), jnp.float32) * STD
        return {'x': x, 'W_up': W_up, 'W_gate': W_gate, 'W_down': W_down, 'gate_inp': gate_inp}
    _L0_ffn_in = _L0_ffn_setup()
    _d = {'L0_attn_x': _L0_attn_in['x'], 'L0_attn_Wq': _L0_attn_in['Wq'], 'L0_attn_Wk': _L0_attn_in['Wk'], 'L0_attn_Wv': _L0_attn_in['Wv'], 'L0_attn_Wa': _L0_attn_in['Wa'], 'L0_attn_ba': _L0_attn_in['ba'], 'L0_attn_Wb': _L0_attn_in['Wb'], 'L0_attn_bb': _L0_attn_in['bb'], 'L0_attn_Wg': _L0_attn_in['Wg'], 'L0_attn_Wo': _L0_attn_in['Wo'], 'L0_attn_qc_w': _L0_attn_in['qc_w'], 'L0_attn_qc_b': _L0_attn_in['qc_b'], 'L0_attn_kc_w': _L0_attn_in['kc_w'], 'L0_attn_kc_b': _L0_attn_in['kc_b'], 'L0_attn_vc_w': _L0_attn_in['vc_w'], 'L0_attn_vc_b': _L0_attn_in['vc_b'], 'L0_attn_ln_g': _L0_attn_in['ln_g'], 'L0_attn_ln_b': _L0_attn_in['ln_b'], 'L0_ffn_W_up': _L0_ffn_in['W_up'], 'L0_ffn_W_gate': _L0_ffn_in['W_gate'], 'L0_ffn_W_down': _L0_ffn_in['W_down'], 'L0_ffn_gate_inp': _L0_ffn_in['gate_inp']}
    _x0 = _d['L0_attn_x']
    _d['L0_attn_x'] = jax.random.normal(jax.random.fold_in(jax.random.key(seed), 1), (1, 2048, 256), dtype=_x0.dtype)
    del _x0
    return _d

def reference(L0_attn_x, L0_attn_Wq, L0_attn_Wk, L0_attn_Wv, L0_attn_Wa, L0_attn_ba, L0_attn_Wb, L0_attn_bb, L0_attn_Wg, L0_attn_Wo, L0_attn_qc_w, L0_attn_qc_b, L0_attn_kc_w, L0_attn_kc_b, L0_attn_vc_w, L0_attn_vc_b, L0_attn_ln_g, L0_attn_ln_b, L0_ffn_W_up, L0_ffn_W_gate, L0_ffn_W_down, L0_ffn_gate_inp):

    def _L0_attn_ref(x, Wq, Wk, Wv, Wa, ba, Wb, bb, Wg, Wo, qc_w, qc_b, kc_w, kc_b, vc_w, vc_b, ln_g, ln_b):
        import jax, jax.numpy as jnp
        import numpy as np
        B, S, HID = (1, 128, 256)
        H, DQK, DV = (16, 128, 128)
        K = 4
        SCALE = DQK ** (-0.5)

        def _dwconv_causal(x_btc, wk, bk, seq):
            y = jax.lax.conv_general_dilated(x_btc.transpose(0, 2, 1), wk, (1,), [(K - 1, K - 1)], dimension_numbers=('NCH', 'OIH', 'NCH'), feature_group_count=wk.shape[0])
            return (y[:, :, :seq] + bk[None, :, None]).transpose(0, 2, 1)

        def _kda_forward(x, Wq, Wk, Wv, Wa, ba, Wb, bb, Wg, Wo, qc_w, qc_b, kc_w, kc_b, vc_w, vc_b, ln_g, ln_b):
            Bb, Ss, _ = x.shape
            q = x @ Wq.T
            k = x @ Wk.T
            v = x @ Wv.T
            q = jax.nn.silu(_dwconv_causal(q, qc_w, qc_b, Ss))
            k = jax.nn.silu(_dwconv_causal(k, kc_w, kc_b, Ss))
            v = jax.nn.silu(_dwconv_causal(v, vc_w, vc_b, Ss))
            q = q.reshape(Bb, Ss, H, DQK)
            k = k.reshape(Bb, Ss, H, DQK) * SCALE
            v = v.reshape(Bb, Ss, H, DV)
            a = jax.nn.sigmoid(x @ Wa.T + ba).reshape(Bb, Ss, H, DV)
            beta = jax.nn.sigmoid(x @ Wb.T + bb)

            def step(St, inp):
                kt, qt, vt, at, bt = inp
                Sk = jnp.einsum('bhij,bhj->bhi', St, kt)
                err = Sk - vt
                Sn = at[..., None] * St - (bt[..., None] * err)[..., None] * kt[:, :, None, :]
                ot = jnp.einsum('bhij,bhj->bhi', Sn, qt)
                return (Sn, ot)
            tfirst = lambda u: u.transpose(1, 0, 2, 3)
            S0 = jnp.zeros((Bb, H, DV, DQK), x.dtype)
            _, outs = jax.lax.scan(step, S0, (tfirst(k), tfirst(q), tfirst(v), tfirst(a), beta.transpose(1, 0, 2)))
            out = outs.transpose(1, 0, 2, 3)
            mu = out.mean(-1, keepdims=True)
            var = out.var(-1, keepdims=True)
            o = (out - mu) * jax.lax.rsqrt(var + 1e-05) * ln_g + ln_b
            g = jax.nn.sigmoid(x @ Wg.T).reshape(Bb, Ss, H, DV)
            o = (o * g).reshape(Bb, Ss, H * DV)
            return o @ Wo.T
        return _kda_forward(x, Wq, Wk, Wv, Wa, ba, Wb, bb, Wg, Wo, qc_w, qc_b, kc_w, kc_b, vc_w, vc_b, ln_g, ln_b)

    def _L0_ffn_ref(x, W_up, W_gate, W_down, gate_inp):
        import jax, jax.numpy as jnp
        import numpy as np
        E, K = (16, 4)
        C, H = (256, 448)
        B, T = (2, 64)
        STD = 0.02
        b, t, c = x.shape
        xf = x.reshape(b * t, c)
        logits = xf @ gate_inp.T
        topv, topi = jax.lax.top_k(logits, K)
        w = jax.nn.softmax(topv.astype(jnp.float32), axis=-1).astype(x.dtype)
        n = xf.shape[0]
        dense_w = jnp.zeros((n, E), x.dtype).at[jnp.arange(n)[:, None], topi].set(w)
        u = jnp.einsum('nc,ehc->neh', xf, W_up)
        g = jnp.einsum('nc,ehc->neh', xf, W_gate)
        h = jax.nn.silu(g) * u
        y = jnp.einsum('neh,ech,ne->nc', h, W_down, dense_w)
        return y.reshape(b, t, c)
    x = L0_attn_x
    xn = _layernorm(x, axis=-1)
    x = x + _L0_attn_ref(xn, L0_attn_Wq, L0_attn_Wk, L0_attn_Wv, L0_attn_Wa, L0_attn_ba, L0_attn_Wb, L0_attn_bb, L0_attn_Wg, L0_attn_Wo, L0_attn_qc_w, L0_attn_qc_b, L0_attn_kc_w, L0_attn_kc_b, L0_attn_vc_w, L0_attn_vc_b, L0_attn_ln_g, L0_attn_ln_b) + _L0_ffn_ref(xn, L0_ffn_W_up, L0_ffn_W_gate, L0_ffn_W_down, L0_ffn_gate_inp)
    return x

_drawn_inputs = setup_inputs


def setup_inputs(seed=0):
    import zlib

    import numpy as np

    out = dict(_drawn_inputs(seed))
    spreads = {'L0_attn_ba': (0.0, 2.0),
     'L0_attn_bb': (0.0, 2.0),
     'L0_attn_qc_b': (0.0, 0.1),
     'L0_attn_kc_b': (0.0, 0.1),
     'L0_attn_vc_b': (0.0, 0.1),
     'L0_attn_ln_g': (1.0, 0.6),
     'L0_attn_ln_b': (0.0, 0.338)}
    factors = {'L0_attn_Wa': 21.956,
     'L0_attn_Wb': 20.29,
     'L0_attn_Wg': 4.78,
     'L0_ffn_W_up': 4.968,
     'L0_ffn_W_gate': 4.979,
     'L0_ffn_W_down': 4.916,
     'L0_ffn_gate_inp': 5.67}
    for name, (base, spread) in spreads.items():
        noise = np.random.default_rng([zlib.crc32(name.encode()), seed]).standard_normal(out[name].shape)
        drawn = base * np.exp(spread * noise) if base else spread * noise
        out[name] = jnp.asarray(drawn.astype(out[name].dtype))
    for name, factor in factors.items():
        out[name] = (out[name] * factor).astype(out[name].dtype)
    return out
```

```python
from contextlib import ExitStack

import concourse.bass as bass
from concourse import mybir

F32 = mybir.dt.float32
ALU = mybir.AluOpType
ACT = mybir.ActivationFunctionType
AX = mybir.AxisListType

P = 128
S = 2048
HID = 256
KT = HID // P
H = 16
D = 128
TAPS = 4
HALO = TAPS - 1
SCALE = float(D) ** -0.5
EPS = 1e-5
E = 16
TOPK = 4
F = 448
PAIRS = E // 2
FT = 2 * F // P
FH = F - 3 * P
TB = 512
NTB = S // TB
CH = 32
NCH = S // CH
LEAF = 8
NLEAF = CH // LEAF
HT = H * CH
NM = H * NLEAF
TT = S // P
BLK = 128
NBLK = S // BLK
CPB = BLK // CH
K_, Q_, V_, A_, G_ = range(5)
NT = 5
POOL_STEPS = 15
DVE_STEPS = 76


class Counted:

    def __init__(self, sem, per, first=None):
        self.sem, self.per, self.first = sem, per, first or per

    def at(self, r, j):
        return r * self.per + (self.first + j)


def heads(ap, n=H):
    return ap.rearrange("p (h t) -> p h t", h=n)


def build(nc, x, xT, projT, wbT, gateT, convw, chan, bb, lnp, woT, wupT, wgT, wdT, consts, out):
    spill = nc.dram_tensor("spill", (CPB + NCH + 2, P, NT * HT), F32, kind="Internal").ap()
    betas = nc.dram_tensor("betas", (NCH + 2, 1, HT), F32, kind="Internal").ap()
    ospill = nc.dram_tensor("ospill", (NCH + 1, P, HT), F32, kind="Internal").ap()
    with ExitStack() as ctx:
        def sb(name, n, parts=P, c=ctx):
            return c.enter_context(nc.sbuf_tensor(name, [parts, n], F32))

        ps = [ctx.enter_context(nc.psum_tensor(f"bank{i}", [P, 512], F32)) for i in range(8)]
        xn = sb("xn", KT * (HALO + S))
        xn3 = xn[:].rearrange("p (k t) -> p k t", k=KT)
        yacc = sb("yacc", TT * HID)
        cst = sb("cst", 6 * P)
        ident, blk2, blk4, blk8, blk16 = (cst[:, i * P:(i + 1) * P] for i in range(5))
        ties = cst[:, 5 * P:6 * P]
        dense = sb("dense", TT * E)
        chs = sb("chs", 4 * H)
        cw = sb("cw", 3 * H * TAPS)
        lns = sb("lns", 2)
        bbs = sb("bbs", 1, H)
        eps = sb("eps", 1)
        ones = sb("ones", P)
        onesh = sb("onesh", P)
        onesd = sb("onesd", P)
        centre = ties

        norm_phase(nc, ps, x, xT, wbT, gateT, convw, chan, bb, lnp, consts, betas, xn, yacc, cst, dense, chs,
                   cw, lns, bbs, eps, ones, onesh, onesd, ties)
        projection_phase(nc, ps, projT, spill, xn3, chs, cw)
        recurrence_phase(nc, ps, spill, ospill, betas, wupT, wgT, wdT, xn3, yacc, ident, blk2, blk4, blk8, blk16,
                         dense, ones)
        output_phase(nc, ps, spill, ospill, woT, yacc, lns, eps, centre, onesd, out)


def norm_phase(nc, ps, x, xT, wbT, gateT, convw, chan, bb, lnp, consts, betas, xn, yacc, cst, dense, chs,
               cw, lns, bbs, eps, ones, onesh, onesd, ties):
    xn3 = xn[:].rearrange("p (k t) -> p k t", k=KT)
    NB4 = S // 512
    with ExitStack() as ctx:
        def sb(name, n, parts=P):
            return ctx.enter_context(nc.sbuf_tensor(name, [parts, n], F32))

        def sem(name):
            return ctx.enter_context(nc.semaphore(name))

        xr = sb("xr", KT * S)
        xr3 = xr[:].rearrange("p (k t) -> p k t", k=KT)
        sq = sb("sq", KT * S)
        sq3 = sq[:].rearrange("p (k t) -> p k t", k=KT)
        std = sb("std", S)
        nbh = sb("nbh", S + 2 * CH, H)
        wb = sb("wb", KT * H)
        gt = sb("gt", KT * E)
        lg = sb("lg", TT * E)
        cmp_gt = sb("cmp_gt", 4 * E * E)
        cmp_eq = sb("cmp_eq", 4 * E * E)
        rank = sb("rank", TT * E)
        top = sb("top", TT)
        tot = sb("tot", TT)
        x_in = sem("x_in")
        small_in = sem("small_in")
        made = sem("made")
        mean_done = sem("mean_done")
        centred = sem("centred")
        squared = sem("squared")
        var_done = sem("var_done")
        std_done = sem("std_done")
        dve_step = sem("norm_dve_step")
        normed = sem("normed")
        beta_mm = sem("beta_mm")
        beta_sig = sem("beta_sig")
        negated = sem("negated")
        beta_out = sem("beta_out")
        logits_mm = sem("logits_mm")
        shifted = sem("shifted")
        expd = sem("expd")
        block = ctx.enter_context(nc.Block())

        @block.sync
        def _(sp):
            sp.dma_start(xr[:], xT).then_inc(x_in, 16)
            loads = [(cst[:], consts), (wb[:], wbT), (gt[:], gateT), (cw[:], convw), (chs[:], chan),
                     (bbs[:], bb), (lns[:], lnp),
                     (yacc[:].rearrange("p (n c) -> p n c", n=TT), x.rearrange("(n p) c -> p n c", p=P))]
            for dst, src in loads:
                sp.dma_start(dst, src).then_inc(small_in, 16)
            sp.wait_ge(small_in, 16 * len(loads))
            sp.wait_ge(made, 1)
            sp.wait_ge(negated, NB4)
            sp.dma_start(betas.rearrange("c o (h t) -> h (o c) t", h=H),
                         nbh[:].rearrange("h (c t) -> h c t", t=CH)).then_inc(beta_out, 16)
            sp.wait_ge(beta_out, 16)

        @block.gpsimd
        def _(pool):
            pool.memset(ones[:], 1.0)
            pool.memset(onesh[:], 1.0 / HID)
            pool.memset(onesd[:], 1.0 / D)
            pool.memset(eps[:], EPS)
            pool.memset(nbh[:, S:S + 2 * CH], 0.0)
            pool.memset(xn3[:, :, 0:HALO], 0.0).then_inc(made, 1)

        @block.tensor
        def _(pe):
            pe.wait_ge(made, 1)
            pe.wait_ge(x_in, 16)
            for b in range(NB4):
                for k in range(KT):
                    mm = pe.matmul(ps[b][:], onesh[:], xr3[:, k, b * 512:(b + 1) * 512],
                                   start=(k == 0), stop=(k == KT - 1))
                mm.then_inc(mean_done, 1)
            for b in range(NB4):
                pe.wait_ge(squared, b + 1)
                for k in range(KT):
                    mm = pe.matmul(ps[4 + b][:], onesh[:], sq3[:, k, b * 512:(b + 1) * 512],
                                   start=(k == 0), stop=(k == KT - 1))
                mm.then_inc(var_done, 1)
            pe.wait_ge(small_in, 16 * 8)
            for b in range(NB4):
                pe.wait_ge(normed, KT * (b + 1))
                for k in range(KT):
                    mm = pe.matmul(ps[b][0:H, :], wb[:, k * H:(k + 1) * H],
                                   xn3[:, k, HALO + b * 512:HALO + (b + 1) * 512],
                                   start=(k == 0), stop=(k == KT - 1))
                mm.then_inc(beta_mm, 1)
            for t in range(TT):
                for k in range(KT):
                    mm = pe.matmul(ps[4][:, t * E:(t + 1) * E], xn3[:, k, HALO + t * P:HALO + (t + 1) * P],
                                   gt[:, k * E:(k + 1) * E], start=(k == 0), stop=(k == KT - 1))
            mm.then_inc(logits_mm, 1)

        @block.scalar
        def _(act):
            for b in range(NB4):
                act.wait_ge(centred, KT * (b + 1))
                act.activation(sq3[:, :, b * 512:(b + 1) * 512], xr3[:, :, b * 512:(b + 1) * 512],
                               ACT.Square).then_inc(squared, 1)
            for b in range(NB4):
                act.wait_ge(var_done, b + 1)
                act.activation(std[:, b * 512:(b + 1) * 512], ps[4 + b][:], ACT.Sqrt,
                               bias=eps[:, 0:1]).then_inc(std_done, 1)
            for b in range(NB4):
                act.wait_ge(beta_mm, b + 1)
                act.activation(nbh[:, b * 512:(b + 1) * 512], ps[b][0:H, :], ACT.Sigmoid,
                               bias=bbs[:, 0:1]).then_inc(beta_sig, 1)
            act.wait_ge(shifted, 1)
            act.activation(rank[:], lg[:], ACT.Exp).then_inc(expd, 1)

        @block.vector
        def _(dve):
            n = [0]

            def link(ins):
                n[0] += 1
                ins.then_inc(dve_step, 1)
                dve.wait_ge(dve_step, n[0])

            for b in range(NB4):
                dve.wait_ge(mean_done, b + 1)
                for k in range(KT):
                    blk = xr3[:, k, b * 512:(b + 1) * 512]
                    dve.tensor_tensor(blk, blk, ps[b][:], ALU.subtract).then_inc(centred, 1)
            for b in range(NB4):
                blk = std[:, b * 512:(b + 1) * 512]
                dve.wait_ge(std_done, b + 1)
                link(dve.reciprocal(blk, blk))
                for k in range(KT):
                    dve.tensor_tensor(xn3[:, k, HALO + b * 512:HALO + (b + 1) * 512],
                                      xr3[:, k, b * 512:(b + 1) * 512], blk, ALU.mult).then_inc(normed, 1)
            for b in range(NB4):
                blk = nbh[:, b * 512:(b + 1) * 512]
                dve.wait_ge(beta_sig, b + 1)
                dve.tensor_scalar(blk, blk, -1.0, None, ALU.mult).then_inc(negated, 1)
            dve.wait_ge(logits_mm, 1)
            link(dve.tensor_copy(lg[:], ps[4][:, 0:TT * E]))
            tie = ties.rearrange("p (e f) -> p e f", e=8)
            for t0 in range(0, TT, 4):
                g4 = cmp_gt[:].rearrange("p (t e f) -> p t e f", t=4, e=E)
                q4 = cmp_eq[:].rearrange("p (t e f) -> p t e f", t=4, e=E)
                for u in range(4):
                    row = lg[:, (t0 + u) * E:(t0 + u + 1) * E]
                    other = row.unsqueeze(1).broadcast_to([P, E, E])
                    own = row.unsqueeze(2).broadcast_to([P, E, E])
                    dve.tensor_tensor(g4[:, u], other, own, ALU.is_gt)
                    link(dve.tensor_tensor(q4[:, u], other, own, ALU.is_equal))
                    dve.tensor_tensor(q4[:, u, 0:8], q4[:, u, 0:8], tie, ALU.mult)
                    link(dve.tensor_tensor(q4[:, u, 8:16, 8:16], q4[:, u, 8:16, 8:16], tie[:, :, 0:8], ALU.mult))
                link(dve.tensor_tensor(cmp_gt[:], cmp_gt[:], cmp_eq[:], ALU.add))
                link(dve.tensor_reduce(rank[:, t0 * E:(t0 + 4) * E].rearrange("p (t e) -> p t e", t=4),
                                       g4, AX.X, ALU.add))
            dve.tensor_tensor(ties, cst[:, 0:P], onesd[:], ALU.subtract)
            link(dve.tensor_scalar(dense[:], rank[:], float(TOPK), None, ALU.is_lt))
            l3 = lg[:].rearrange("p (t e) -> p t e", t=TT)
            link(dve.tensor_reduce(top[:], l3, AX.X, ALU.max))
            dve.tensor_tensor(l3, l3, top[:].unsqueeze(2).broadcast_to([P, TT, E]),
                              ALU.subtract).then_inc(shifted, 1)
            dve.wait_ge(expd, 1)
            link(dve.tensor_tensor(dense[:], dense[:], rank[:], ALU.mult))
            d3 = dense[:].rearrange("p (t e) -> p t e", t=TT)
            link(dve.tensor_reduce(tot[:], d3, AX.X, ALU.add))
            link(dve.reciprocal(tot[:], tot[:]))
            l4 = lg[:].rearrange("p (t e x) -> p t e x", t=TT, x=2)
            link(dve.tensor_tensor(l3, d3, tot[:].unsqueeze(2).broadcast_to([P, TT, E]), ALU.mult))
            for x in range(2):
                ins = dve.tensor_copy(dense[:, x * PAIRS * TT:(x + 1) * PAIRS * TT].rearrange(
                    "p (e t) -> p t e", e=PAIRS), l4[:, :, :, x])
            link(ins)


def projection_phase(nc, ps, projT, spill, xn3, chs, cw):
    with ExitStack() as ctx:
        def sb(name, n):
            return ctx.enter_context(nc.sbuf_tensor(name, [P, n], F32))

        def sem(name):
            return ctx.enter_context(nc.semaphore(name))

        w = [sb(f"w{i}", KT * H * D) for i in range(NT)]
        w3 = [t[:].rearrange("p (k n) -> p k n", k=KT) for t in w]
        st = [sb(f"st{x}", CPB * NT * HT) for x in range(2)]
        st4 = [t[:].rearrange("p (c x h t) -> p c x h t", c=CPB, x=NT, h=H) for t in st]
        scale = sb("scale", 1)
        w_in = [sem(f"w_in{i}") for i in range(NT)]
        scale_set = sem("scale_set")
        taps_mm = Counted(sem("taps_mm"), H)
        gates_mm = Counted(sem("gates_mm"), H)
        tap3_done = Counted(sem("tap3_done"), 3 * H)
        gates_done = Counted(sem("gates_done"), 2 * H)
        conv_done = Counted(sem("conv_done"), 3 * H)
        conv_step = Counted(sem("conv_step"), 6 * H)
        silu_done = Counted(sem("silu_done"), CPB)
        scaled = Counted(sem("scaled"), CPB)
        out_done = Counted(sem("proj_out"), 16 * CPB)
        block = ctx.enter_context(nc.Block())
        taps_ps = [ps[i][:, 0:3 * (HALO + BLK)].rearrange("p (x t) -> p x t", x=3) for i in range(4)]
        gates_ps = [ps[4 + i][:, 0:2 * BLK].rearrange("p (x t) -> p x t", x=2) for i in range(4)]

        @block.sync
        def _(sp):
            sp.sem_inc(out_done.sem, out_done.per)
            for i in range(NT):
                sp.dma_start(w[i][:], projT[i]).then_inc(w_in[i], 16)
            def store(b, x):
                sp.wait_ge(gates_done.sem, gates_done.at(b, 0))
                for c in range(CPB):
                    sp.wait_ge(scaled.sem, scaled.at(b, c + 1))
                    sp.dma_start(spill[bass.ds(b * CPB + c, 1)].rearrange("c p n -> p (c n)"),
                                 st[x][:, c * NT * HT:(c + 1) * NT * HT]).then_inc(out_done.sem, 16)

            with sp.Fori(0, NBLK // 2) as n:
                for x in range(2):
                    store(n * 2 + x, 1 - x)
            store(NBLK, 1)
            for c in range(2):
                sp.dma_start(spill[CPB + NCH + c], st[1][:, 0:NT * HT]).then_inc(out_done.sem, 16)
            sp.wait_ge(out_done.sem, out_done.at(NBLK + 1, 32))

        @block.tensor
        def _(pe):
            pe.sem_inc(taps_mm.sem, taps_mm.per)
            pe.sem_inc(gates_mm.sem, gates_mm.per)
            for i in range(NT):
                pe.wait_ge(w_in[i], 16)
            with pe.Fori(0, NBLK) as b:
                for h in range(H):
                    pe.wait_ge(conv_done.sem, conv_done.at(b, 3 * (h - 3)))
                    for i in (K_, Q_, V_):
                        for k in range(KT):
                            mm = pe.matmul(taps_ps[h % 4][:, i], w3[i][:, k, h * D:(h + 1) * D],
                                           xn3[:, k, bass.ds(b * BLK, HALO + BLK)],
                                           start=(k == 0), stop=(k == KT - 1))
                    mm.then_inc(taps_mm.sem, 1)
                    pe.wait_ge(gates_done.sem, gates_done.at(b, 2 * (h - 3)))
                    for i in (A_, G_):
                        for k in range(KT):
                            mm = pe.matmul(gates_ps[h % 4][:, i - A_], w3[i][:, k, h * D:(h + 1) * D],
                                           xn3[:, k, bass.ds(b * BLK + HALO, BLK)],
                                           start=(k == 0), stop=(k == KT - 1))
                    mm.then_inc(gates_mm.sem, 1)

        @block.scalar
        def _(act):
            act.sem_inc(tap3_done.sem, tap3_done.per)
            act.sem_inc(gates_done.sem, gates_done.per)
            act.sem_inc(silu_done.sem, silu_done.per)
            act.wait_ge(scale_set, 1)

            def silu(b, x):
                act.wait_ge(conv_done.sem, conv_done.at(b, 0))
                for c in range(CPB):
                    kqv = st[x][:, c * NT * HT:c * NT * HT + 3 * HT]
                    act.activation(kqv, kqv, ACT.Silu).then_inc(silu_done.sem, 1)

            with act.Fori(0, NBLK // 2) as n:
                for x in range(2):
                    b = n * 2 + x
                    act.wait_ge(out_done.sem, out_done.at(b, 0))
                    for h in range(H):
                        act.wait_ge(taps_mm.sem, taps_mm.at(b, h + 1))
                        for i in (K_, Q_, V_):
                            act.activation(st4[x][:, :, i, h], taps_ps[h % 4][:, i, HALO:].rearrange(
                                "p (c t) -> p c t", c=CPB), ACT.Identity, bias=chs[:, i * H + h:i * H + h + 1],
                                scale=cw[:, (i * H + h) * TAPS + HALO:(i * H + h) * TAPS + TAPS]
                            ).then_inc(tap3_done.sem, 1)
                        act.wait_ge(gates_mm.sem, gates_mm.at(b, h + 1))
                        act.activation(st4[x][:, :, A_, h], gates_ps[h % 4][:, 0].rearrange(
                            "p (c t) -> p c t", c=CPB), ACT.Sigmoid, bias=chs[:, 3 * H + h:3 * H + h + 1]
                        ).then_inc(gates_done.sem, 1)
                        act.activation(st4[x][:, :, G_, h], gates_ps[h % 4][:, 1].rearrange(
                            "p (c t) -> p c t", c=CPB), ACT.Sigmoid).then_inc(gates_done.sem, 1)
                        if h == 3:
                            silu(b, 1 - x)
            silu(NBLK, 1)

        @block.vector
        def _(dve):
            dve.sem_inc(conv_done.sem, conv_done.per)
            dve.sem_inc(conv_step.sem, conv_step.per)
            with dve.Fori(0, NBLK // 2) as n:
                for x in range(2):
                    b = n * 2 + x
                    for h in range(H):
                        dve.wait_ge(tap3_done.sem, tap3_done.at(b, 3 * h + 3))
                        for tap in (2, 1, 0):
                            for i in (K_, Q_, V_):
                                acc = st4[x][:, :, i, h]
                                if tap < 2:
                                    dve.wait_ge(conv_step.sem, conv_step.at(b, 6 * h + 3 * (1 - tap) + i + 1))
                                w0 = (i * H + h) * TAPS + tap
                                ins = dve.scalar_tensor_tensor(
                                    out=acc, in0=taps_ps[h % 4][:, i, tap:tap + BLK].rearrange(
                                        "p (c t) -> p c t", c=CPB),
                                    scalar=cw[:, w0:w0 + 1], in1=acc, op0=ALU.mult, op1=ALU.add)
                                ins.then_inc(conv_step.sem if tap else conv_done.sem, 1)

        @block.gpsimd
        def _(pool):
            pool.sem_inc(scaled.sem, scaled.per)
            pool.memset(st[1][:], 0.0)
            pool.memset(scale[:], SCALE).then_inc(scale_set, 1)
            pool.wait_ge(scale_set, 1)

            def scale_k(b, x):
                for c in range(CPB):
                    pool.wait_ge(silu_done.sem, silu_done.at(b, c + 1))
                    k = st[x][:, c * NT * HT:c * NT * HT + HT]
                    pool.tensor_tensor(k, k, scale[:].broadcast_to([P, HT]), ALU.mult).then_inc(scaled.sem, 1)

            with pool.Fori(0, NBLK // 2) as n:
                for x in range(2):
                    scale_k(n * 2 + x, 1 - x)
            scale_k(NBLK, 1)


def recurrence_phase(nc, ps, spill, ospill, betas, wupT, wgT, wdT, xn3, yacc, ident, blk2, blk4, blk8, blk16, dense,
                     ones):
    bank_z = ps[0:2]
    bank_t, bank_c, bank_p = ps[2], ps[3], ps[4]
    bank_gate, bank_up, bank_y = ps[5], ps[6], ps[7]
    leaf_bank = (bank_p, bank_z[0])
    FILLS = [(0, 6), (1, 5), (2, 4), (3,)]
    COL, LM = {}, 0
    for js in FILLS:
        for j in js:
            COL[j] = LM
            LM += NM * (LEAF - 1 - j)

    def column(ap, j, base=0):
        n = LEAF - 1 - j
        return ap[:, COL[j] - base:COL[j] - base + NM * n].rearrange("p (m t) -> p m t", t=n)

    SLOTS = 8
    CARRY = NTB

    with ExitStack() as ctx:
        def sb(name, n, parts=P):
            return ctx.enter_context(nc.sbuf_tensor(name, [parts, n], F32))

        def counted(name, per):
            return Counted(ctx.enter_context(nc.semaphore(name)), per)

        def two(name, n):
            return [sb(f"{name}{c}", n) for c in range(2)]

        inb = two("inb", 4 * HT)
        leafm = two("leafm", LM)
        decay = sb("decay", LM)
        nb = two("nb", HT)
        pre = {m: two(f"pre{m}_", HT // 2) for m in (2, 4, 8, 16)}
        suf = {m: two(f"suf{m}_", HT // 2) for m in (2, 4, 8, 16)}
        prec = sb("prec", HT)
        sufc = two("sufc", HT)
        tot = two("tot", H)
        kc = {m: sb(f"kc{m}_", HT // 2) for m in (2, 4, 8, 16)}
        gram = two("gram", 4 * 2 * P)
        grams = two("grams", 6 * P)
        kq = two("kq", HT)
        prod = two("prod", 512)
        runa = {m: sb(f"runa{m}", H * CH // m) for m in (2, 4, 8, 16)}
        runs = sb("runs", HT)
        z = sb("z", HT)
        zq = sb("zq", HT)
        w = z
        tmp = sb("tmp", HT)
        tmpq = sb("tmpq", HT)
        uc = sb("uc", HT)
        u8 = [uc[:, 0:H * 8], uc[:, H * 8:H * 16]]
        u16 = uc[:, H * 16:H * 32]
        us = tmpq
        uts = sb("uts", 6 * P)
        ut = uts[:, 0:2 * P]
        utc = tmp
        a_cur = sb("a_cur", HT)
        kn = sb("kn", 4 * 512)
        kn4 = kn[:].rearrange("p (g h d) -> p g h d", g=4, h=4)
        st = sb("state", H * D)
        stT = sb("stateT", H * D)
        ob = sb("ob", HT)
        wu = sb("wu", FT * KT * P)
        wg = sb("wg", FT * KT * P)
        wd = sb("wd", FT * HID)
        hT = sb("hT", FT * TB)

        in_done = [ctx.enter_context(nc.semaphore(f"in_done{c}")) for c in range(2)]
        nb_done = [ctx.enter_context(nc.semaphore(f"nb_done{c}")) for c in range(2)]
        o_out = counted("o_out", 16)
        z_mm = counted("z_mm", 2)
        ktr_mm = counted("ktr_mm", 1)
        prep_mm = counted("prep_mm", 8)
        kq_mm = counted("kq_mm", 1)
        ut_mm = counted("ut_mm", 4)
        c_mm = counted("c_mm", 3)
        s_mm = counted("s_mm", 4)
        st_mm = counted("st_mm", 4)
        uts_mm = counted("uts_mm", 1)
        cs_mm = counted("cs_mm", 1)
        kn_cp = counted("kn_cp", 4)
        a_cp = counted("a_cp", 1)
        kc_cp = counted("kc_cp", 1)
        kq_cp = counted("kq_cp", 1)
        ut_cp = counted("ut_cp", 4)
        st_cp = counted("st_cp", 4)
        uts_cp = counted("uts_cp", 1)
        z_ready = counted("z_ready", 2)
        u_ready = counted("u_ready", 4)
        us_ready = counted("us_ready", 1)
        prep_used = counted("prep_used", 8)
        c_used = counted("c_used", 3)
        s_ready = counted("s_ready", 4)
        cs_used = counted("cs_used", 1)
        o_ready = counted("o_ready", 1)
        dve_step = counted("dve_step", DVE_STEPS)
        prod_ready = counted("prod_ready", 5)
        decay_ready = counted("decay_ready", 1)
        span_ready = counted("span_ready", 1)
        pool_step = counted("pool_step", POOL_STEPS)
        ffn_mm = counted("ffn_mm", FT)
        silu_done = counted("silu_done", FT)
        h_done = counted("h_done", FT)
        y_mm = counted("y_mm", SLOTS)
        y_used = counted("y_used", SLOTS)
        wgu_in = [ctx.enter_context(nc.semaphore(f"wgu_in{i}")) for i in range(FT)]
        wd_in = [ctx.enter_context(nc.semaphore(f"wd_in{i}")) for i in range(2)]
        cleared = ctx.enter_context(nc.semaphore("cleared"))
        block = ctx.enter_context(nc.Block())

        def halves(ap, m, half):
            return ap.rearrange("p (n x m) -> p n x m", x=2, m=m)[:, :, half]

        def blocks(ap, m):
            return ap.rearrange("p (n m) -> p n m", m=m)

        @block.sync
        def _(sp):
            def load_gu(i, src_up, src_gate):
                sp.dma_start(wu[:, i * 2 * P:(i + 1) * 2 * P], src_up).then_inc(wgu_in[i], 16)
                sp.dma_start(wg[:, i * 2 * P:(i + 1) * 2 * P], src_gate).then_inc(wgu_in[i], 16)

            def load_d(i, row):
                lo, hi = (0, 3) if i == 0 else (3, FT)
                sp.dma_start(wd[:, lo * HID:hi * HID], row[:, lo * HID:hi * HID]).then_inc(wd_in[i], 16)

            for i in range(FT):
                cols = slice(i * 2 * P, (i + 1) * 2 * P)
                load_gu(i, wupT[0][:, cols], wgT[0][:, cols])
            for i in range(2):
                load_d(i, wdT[0])
            with sp.Fori(0, PAIRS - 1) as p:
                last = p * NTB + (NTB - 1)

                def row(t):
                    return t[bass.ds(p + 1, 1)].rearrange("o p n -> p (o n)")

                for i in range(FT):
                    sp.wait_ge(ffn_mm.sem, ffn_mm.at(last, i + 1))
                    cols = slice(i * 2 * P, (i + 1) * 2 * P)
                    load_gu(i, row(wupT)[:, cols], row(wgT)[:, cols])
                sp.wait_ge(y_mm.sem, y_mm.at(last, SLOTS))
                load_d(0, row(wdT))
                sp.wait_ge(y_mm.sem, y_mm.at(last + 1, CARRY))
                load_d(1, row(wdT))
            for i in range(FT):
                sp.wait_ge(wgu_in[i], 32 * PAIRS)
            for s in wd_in:
                sp.wait_ge(s, 16 * PAIRS)

        def htile(j):
            return hT[:, j * TB:(j + 1) * TB]

        @block.gpsimd
        def _(pool):
            for s in (prod_ready, decay_ready, span_ready, pool_step):
                pool.sem_inc(s.sem, s.per)
            pool.memset(kn[:], 0.0)
            pool.memset(ob[:], 0.0)
            pool.memset(decay[:], 1.0)
            pool.memset(hT[:], 0.0)
            pool.memset(stT[:], 0.0)
            pool.memset(st[:], 0.0).then_inc(cleared, 1)

            def prepare(r, c, turn, first=False):
                k, q = inb[c][:, 0:HT], inb[c][:, HT:2 * HT]
                a = inb[c][:, 3 * HT:4 * HT]
                step = [0]

                def link(ins):
                    step[0] += 1
                    ins.then_inc(pool_step.sem, 1)
                    pool.wait_ge(pool_step.sem, pool_step.at(r, step[0]))

                if not first:
                    pool.wait_ge(o_ready.sem, o_ready.at(r, -1))
                pool.wait_ge(in_done[c], turn * 16 + 16)
                pool.wait_ge(nb_done[c], turn * 16 + 16)
                kl, bl, al = blocks(k, LEAF), blocks(runs[:], LEAF), blocks(a, LEAF)
                pool.wait_ge(span_ready.sem, span_ready.at(r, 0))
                link(pool.tensor_tensor(runs[:], k, nb[c][:], ALU.mult))

                def products(f):
                    for j in FILLS[f]:
                        n = LEAF - 1 - j
                        ins = pool.tensor_tensor(column(prod[f % 2], j, COL[FILLS[f][0]]),
                                                 bl[:, :, j:j + 1].broadcast_to([P, NM, n]),
                                                 kl[:, :, j + 1:LEAF], ALU.mult)
                    ins.then_inc(prod_ready.sem, 1)

                pool.wait_ge(kq_mm.sem, kq_mm.at(r, 0))
                products(0)
                pool.wait_ge(prep_mm.sem, prep_mm.at(r, 4 - 8))
                products(1)
                pool.wait_ge(prep_used.sem, prep_used.at(r, 4 - 8))
                for j in range(LEAF - 3, -1, -1):
                    n = LEAF - 2 - j
                    ins = pool.tensor_tensor(column(decay, j)[:, :, 1:], column(decay, j + 1),
                                             al[:, :, j + 1:j + 2].broadcast_to([P, NM, n]), ALU.mult)
                    if j:
                        link(ins)
                ins.then_inc(decay_ready.sem, 1)
                pool.wait_ge(prep_mm.sem, prep_mm.at(r, 1))
                products(2)
                pool.wait_ge(prep_mm.sem, prep_mm.at(r, 2))
                products(3)
                if not first:
                    pool.wait_ge(z_ready.sem, z_ready.at(r, 2 - 2))
                pool.wait_ge(prod_ready.sem, prod_ready.at(r, 4))
                even, odd = halves(a, 1, 0), halves(a, 1, 1)
                pool.tensor_tensor(blocks(runa[2][:], 1), even, odd, ALU.mult)
                pool.memset(halves(prec[:], 1, 0), 1.0)
                pool.memset(halves(runs[:], 1, 1), 1.0)
                pool.tensor_copy(halves(prec[:], 1, 1), even)
                link(pool.tensor_copy(halves(runs[:], 1, 0), odd))
                m = 2
                while m < CH:
                    nblk = H * CH // m
                    whole = runa[m][:].rearrange("p (n x) -> p n x", x=2)
                    dst = tot[c] if m == CH // 2 else runa[2 * m]
                    pool.tensor_tensor(blocks(dst[:], 1), whole[:, :, 0:1], whole[:, :, 1:2], ALU.mult)
                    pool.tensor_copy(blocks(pre[m][c][:], m), halves(prec[:], m, 1))
                    if m < LEAF:
                        link(pool.tensor_copy(blocks(suf[m][c][:], m), halves(runs[:], m, 0)))
                    else:
                        link(pool.tensor_tensor(blocks(suf[m][c][:], m), halves(runs[:], m, 0),
                                                halves(nb[c][:], m, 0), ALU.mult))
                    pool.tensor_tensor(halves(prec[:], m, 1), halves(prec[:], m, 1),
                                       whole[:, :, 0:1].broadcast_to([P, nblk // 2, m]), ALU.mult)
                    link(pool.tensor_tensor(halves(runs[:], m, 0), halves(runs[:], m, 0),
                                            whole[:, :, 1:2].broadcast_to([P, nblk // 2, m]), ALU.mult))
                    if m == 4:
                        pool.wait_ge(prep_mm.sem, prep_mm.at(r, 3))
                        pool.tensor_tensor(prod[0][:], k, q, ALU.mult).then_inc(prod_ready.sem, 1)
                    m *= 2
                pool.tensor_tensor(sufc[c][:], runs[:], nb[c][:], ALU.mult).then_inc(span_ready.sem, 1)
                assert step[0] == POOL_STEPS

            prepare(0, 0, 0, first=True)
            with pool.Fori(0, PAIRS) as p, pool.Fori(0, NTB) as b:
                n = p * NTB + b
                for c in range(2):
                    m = n * 2 + c
                    prepare(m + 1, 1 - c, n + c)

        @block.tensor
        def _(pe):
            for s in (z_mm, ktr_mm, prep_mm, kq_mm, ut_mm, c_mm, s_mm, st_mm, uts_mm, cs_mm, ffn_mm, y_mm):
                pe.sem_inc(s.sem, s.per)

            def leaf_dots(r, f):
                pe.wait_ge(prod_ready.sem, prod_ready.at(r, f + 1))
                if f >= 2:
                    pe.wait_ge(prep_used.sem, prep_used.at(r, f - 1))
                cols = sum(NM * (LEAF - 1 - j) for j in FILLS[f])
                pe.matmul(leaf_bank[f % 2][:, 0:cols], ones[:], prod[f % 2][:, 0:cols],
                          start=True, stop=True).then_inc(prep_mm.sem, 1)

            def kq_dots(r):
                pe.wait_ge(prod_ready.sem, prod_ready.at(r, 5))
                pe.wait_ge(prep_used.sem, prep_used.at(r, 3))
                pe.matmul(bank_p[:], ones[:], prod[0][:], start=True, stop=True).then_inc(kq_mm.sem, 1)

            def kq3(c):
                return inb[c][:, 0:2 * HT].rearrange("p (x h t) -> p x h t", x=2, h=H)

            def gram8(r, c):
                pe.wait_ge(prep_used.sem, prep_used.at(r, 4))
                pe.wait_ge(kc_cp.sem, kc_cp.at(r, 1))
                for o in range(2):
                    t = o * 16
                    mm = pe.matmul(bank_z[0][:, o * 256:(o + 1) * 256], kc[8][:, o * P:(o + 1) * P],
                                   kq3(c)[:, :, :, t + 8:t + 16], start=True, stop=True)
                mm.then_inc(prep_mm.sem, 1)

            def gram16(r, c):
                pe.wait_ge(kq_cp.sem, kq_cp.at(r, 1))
                for g in range(2):
                    mm = pe.matmul(bank_p[:, g * 256:(g + 1) * 256], kc[16][:, g * P:(g + 1) * P],
                                   kq3(c)[:, :, 8 * g:8 * g + 8, 16:32], start=True, stop=True)
                mm.then_inc(prep_mm.sem, 1)

            def gram_small(r, c, levels, use):
                pe.wait_ge(prep_used.sem, prep_used.at(r, use))
                for i, m in enumerate(levels):
                    for g in range(2):
                        mm = pe.matmul(bank_p[:, (2 * i + g) * P:(2 * i + g + 1) * P],
                                       kc[m][:, g * P:(g + 1) * P] if m > 1 else
                                       inb[c][:, g * 256:(g + 1) * 256].rearrange("p (n x) -> p x n", x=2)[:, 0],
                                       halves(inb[c][:, HT + g * 256:HT + (g + 1) * 256], m, 1),
                                       start=True, stop=True)
                mm.then_inc(prep_mm.sem, 1)

            def experts(p, n, b, slot):
                if slot == 3:
                    output(p, n, slot)
                if slot < FT:
                    pe.wait_ge(wgu_in[slot], p * 32 + 32)
                    pe.wait_ge(h_done.sem, h_done.at(n, slot))
                    if slot % 4 == 0:
                        pe.wait_ge(cs_used.sem, cs_used.at(n * 2 + slot // 4, 0))
                    for bank, wt in ((bank_gate, wg), (bank_up, wu)):
                        for k in range(KT):
                            mm = pe.matmul(bank[:], wt[:, (slot * KT + k) * P:(slot * KT + k + 1) * P],
                                           xn3[:, k, bass.ds(b * TB + HALO, TB)],
                                           start=(k == 0), stop=(k == KT - 1))
                    mm.then_inc(ffn_mm.sem, 1)
                if slot != 3:
                    output(p, n, slot)

            def output(p, n, slot):
                second, unit = slot < CARRY, n - 1 if slot < CARRY else n
                if slot == CARRY:
                    for s in wd_in:
                        pe.wait_ge(s, p * 16 + 16)
                pe.wait_ge(y_used.sem, y_used.at(n, slot))
                pe.wait_ge(h_done.sem, h_done.at(unit, FT if second else 4))
                tok = slot % CARRY * P
                rows = [(j, 0, P) for j in range(4, FT)] + [(3, FH, P)] if second else \
                    [(j, 0, P) for j in range(3)] + [(3, 0, FH)]
                for i, (j, lo, hi) in enumerate(rows):
                    mm = pe.matmul(bank_y[:, 0:HID], htile(j)[lo:hi, tok:tok + P],
                                   wd[lo:hi, j * HID:(j + 1) * HID],
                                   start=(i == 0), stop=(i == len(rows) - 1))
                mm.then_inc(y_mm.sem, 1)

            def level_turn(m, i, src, groups):
                pe.wait_ge(u_ready.sem, u_ready.at(m, i))
                if i > 1:
                    pe.wait_ge(ut_cp.sem, ut_cp.at(m, i - 1))
                for g in range(groups):
                    mm = pe.transpose(bank_t[:, g * P:(g + 1) * P], src[:, g * P:(g + 1) * P], ident)
                mm.then_inc(ut_mm.sem, 1)

            def level_sum(m, i, c, first, groups):
                pe.wait_ge(ut_cp.sem, ut_cp.at(m, i))
                if i == 1:
                    pe.wait_ge(cs_used.sem, cs_used.at(m, 0))
                else:
                    pe.wait_ge(c_used.sem, c_used.at(m, i - 1))
                for g in range(groups):
                    mm = pe.matmul(bank_c[:, g * 256:(g + 1) * 256], ut[:, g * P:(g + 1) * P],
                                   gram[c][:, (first + g) * 256:(first + g + 1) * 256], start=True, stop=True)
                mm.then_inc(c_mm.sem, 1)

            pe.wait_ge(cleared, 1)
            pe.wait_ge(in_done[0], 16)
            pe.wait_ge(wd_in[1], 16)
            for f in range(4):
                leaf_dots(0, f)
            kq_dots(0)
            gram8(0, 0)
            gram16(0, 0)
            gram_small(0, 0, (1, 2), 6)
            gram_small(0, 0, (4,), 7)
            with pe.Fori(0, PAIRS) as p, pe.Fori(0, NTB) as b:
                n = p * NTB + b
                for c in range(2):
                    m = n * 2 + c
                    r, rc = m + 1, 1 - c
                    pe.wait_ge(st_cp.sem, st_cp.at(m, 0))
                    pe.wait_ge(s_ready.sem, s_ready.at(m, 0))
                    for h in range(H):
                        mm = pe.matmul(bank_z[h // 8][:, (h % 8) * 64:(h % 8 + 1) * 64].rearrange(
                            "p (x t) -> p x t", x=2), stT[:, h * D:(h + 1) * D],
                            kq3(c)[:, :, h, :], start=True, stop=True)
                        if h % 8 == 7:
                            mm.then_inc(z_mm.sem, 1)
                    pe.wait_ge(prep_used.sem, prep_used.at(m, 8))
                    for g in range(4):
                        mm = pe.transpose(bank_p[:, g * P:(g + 1) * P], inb[c][:, g * P:(g + 1) * P], ident)
                    mm.then_inc(ktr_mm.sem, 1)
                    experts(p, n, b, 4 * c)
                    level_turn(m, 1, u8[0], 1)
                    pe.wait_ge(kn_cp.sem, kn_cp.at(m, 4))
                    leaf_dots(r, 0)
                    level_sum(m, 1, c, 0, 1)
                    pe.wait_ge(z_ready.sem, z_ready.at(m, 2))
                    leaf_dots(r, 1)
                    experts(p, n, b, 4 * c + 1)
                    level_turn(m, 2, u16, 2)
                    leaf_dots(r, 2)
                    level_sum(m, 2, c, 2, 2)
                    leaf_dots(r, 3)
                    experts(p, n, b, 4 * c + 2)
                    level_turn(m, 3, u8[1], 1)
                    kq_dots(r)
                    level_sum(m, 3, c, 1, 1)
                    pe.wait_ge(in_done[rc], (n + c) * 16 + 16)
                    gram8(r, rc)
                    experts(p, n, b, 4 * c + 3)
                    level_turn(m, 4, uc, 4)
                    gram16(r, rc)
                    pe.wait_ge(ut_cp.sem, ut_cp.at(m, 4))
                    pe.wait_ge(prep_used.sem, prep_used.at(r, 5))

                    def state_sum(g):
                        pe.matmul(bank_z[g % 2][:], utc[:, g * P:(g + 1) * P], kn[:, g * 512:(g + 1) * 512],
                                  start=True, stop=True).then_inc(s_mm.sem, 1)

                    state_sum(0)
                    state_sum(1)
                    pe.wait_ge(us_ready.sem, us_ready.at(m, 1))
                    pe.wait_ge(h_done.sem, h_done.at(n, FT if c else 4))
                    for g in range(2):
                        pe.transpose(bank_t[:, g * P:(g + 1) * P], w[:, g * 256:(g + 1) * 256].rearrange(
                            "p (n x) -> p x n", x=2)[:, 0], ident)
                    for g in range(2):
                        pe.transpose(bank_t[:, (2 + g) * P:(3 + g) * P], us[:, g * P:(g + 1) * P], ident)
                    for g in range(2):
                        mm = pe.transpose(bank_up[:, g * P:(g + 1) * P], us[:, (2 + g) * P:(3 + g) * P], ident)
                    mm.then_inc(uts_mm.sem, 1)
                    for g in range(2):
                        pe.wait_ge(s_ready.sem, s_ready.at(m, g + 1))
                        state_sum(2 + g)
                    gram_small(r, rc, (1, 2), 6)
                    pe.wait_ge(uts_cp.sem, uts_cp.at(m, 1))
                    pe.wait_ge(c_used.sem, c_used.at(m, 3))
                    for g in range(6):
                        dst = bank_c[:, g * P:(g + 1) * P] if g < 4 else bank_gate[:, (g - 4) * P:(g - 3) * P]
                        mm = pe.matmul(dst, uts[:, g * P:(g + 1) * P], grams[c][:, g * P:(g + 1) * P],
                                       start=True, stop=True)
                    mm.then_inc(cs_mm.sem, 1)
                    for g in range(4):
                        pe.wait_ge(s_ready.sem, s_ready.at(m, g + 1))
                        if g >= 2:
                            pe.wait_ge(st_cp.sem, st_cp.at(m, g - 1))
                        bank = bank_up if g % 2 else bank_t
                        for x in range(4):
                            mm = pe.transpose(bank[:, x * P:(x + 1) * P],
                                              st[:, (4 * g + x) * D:(4 * g + x + 1) * D], ident)
                        mm.then_inc(st_mm.sem, 1)
                    gram_small(r, rc, (4,), 7)
            for slot in range(CARRY):
                output(PAIRS, PAIRS * NTB, slot)

        @block.scalar
        def _(act):
            for s in (o_out, kn_cp, a_cp, kc_cp, kq_cp, ut_cp, st_cp, uts_cp, silu_done):
                act.sem_inc(s.sem, s.per)

            def copy(dst, src):
                return act.copy(dst, src)

            def load(c, row):
                act.dma_start(inb[c][:], row.rearrange("o p n -> p (o n)")[:, 0:4 * HT]).then_inc(in_done[c], 16)

            def load_beta(c, m):
                act.dma_start(nb[c][:], betas[bass.ds(m, 1)].rearrange("o p n -> p (o n)").broadcast_to([P, HT])
                              ).then_inc(nb_done[c], 16)

            def kq_dots(r, c):
                act.wait_ge(kq_mm.sem, kq_mm.at(r, 1))
                copy(kq[c][:], bank_p[:]).then_inc(kq_cp.sem, 1)

            def experts(n, slot):
                if slot < FT:
                    act.wait_ge(ffn_mm.sem, ffn_mm.at(n, slot + 1))
                    act.wait_ge(y_mm.sem, y_mm.at(n, 0 if slot < 3 else CARRY))
                    act.activation(htile(slot), bank_gate[:], ACT.Silu).then_inc(silu_done.sem, 1)

            def turned(m, i, cols):
                act.wait_ge(ut_mm.sem, ut_mm.at(m, i))
                copy((utc if i == 4 else ut)[:, 0:cols], bank_t[:, 0:cols]).then_inc(ut_cp.sem, 1)

            def store(row):
                act.dma_start(ospill[bass.ds(row, 1)].rearrange("o p n -> p (o n)"), ob[:]
                              ).then_inc(o_out.sem, 16)

            def compact(c, turn):
                act.wait_ge(in_done[c], turn * 16 + 16)
                k = inb[c][:, 0:HT]
                copy(kc[8][:].rearrange("p (o h t) -> p o h t", o=2, h=H),
                     k.rearrange("p (h o x t) -> p x o h t", h=H, o=2, x=2)[:, 0])
                for m in (2, 4, 16):
                    ins = copy(blocks(kc[m][:], m), halves(k, m, 0))
                ins.then_inc(kc_cp.sem, 1)

            for c in range(2):
                load(c, spill[CPB + c:CPB + c + 1])
                load_beta(c, c)
            act.wait_ge(cleared, 1)
            compact(0, 0)
            kq_dots(0, 0)
            with act.Fori(0, PAIRS) as p, act.Fori(0, NTB) as b:
                n = p * NTB + b
                for c in range(2):
                    m = n * 2 + c
                    act.wait_ge(ktr_mm.sem, ktr_mm.at(m, 1))
                    for x in range(4):
                        rows = slice(x * CH, (x + 1) * CH)
                        copy(kn4[rows, :, x], bank_p[rows, :].rearrange("p (g d) -> p g d", g=4)
                             ).then_inc(kn_cp.sem, 1)
                    act.wait_ge(o_ready.sem, o_ready.at(m, 0))
                    copy(a_cur[:], inb[c][:, 3 * HT:4 * HT]).then_inc(a_cp.sem, 1)
                    store(m)
                    act.wait_ge(z_ready.sem, z_ready.at(m, 2))
                    act.wait_ge(a_cp.sem, a_cp.at(m, 1))
                    load(c, spill[bass.ds(m + (CPB + 2), 1)])
                    compact(1 - c, n + c)
                    experts(n, 4 * c)
                    turned(m, 1, P)
                    experts(n, 4 * c + 1)
                    turned(m, 2, 2 * P)
                    experts(n, 4 * c + 2)
                    turned(m, 3, P)
                    kq_dots(m + 1, 1 - c)
                    experts(n, 4 * c + 3)
                    turned(m, 4, 4 * P)
                    act.wait_ge(us_ready.sem, us_ready.at(m, 1))
                    load_beta(c, m + 2)
                    act.wait_ge(uts_mm.sem, uts_mm.at(m, 1))
                    copy(uts[:, 0:4 * P], bank_t[:])
                    copy(uts[:, 4 * P:6 * P], bank_up[:, 0:2 * P]).then_inc(uts_cp.sem, 1)
                    for g in range(4):
                        act.wait_ge(st_mm.sem, st_mm.at(m, g + 1))
                        copy(stT[:, g * 512:(g + 1) * 512], (bank_up if g % 2 else bank_t)[:]
                             ).then_inc(st_cp.sem, 1)
            act.wait_ge(o_ready.sem, o_ready.at(NCH, 0))
            store(NCH)
            act.wait_ge(o_out.sem, o_out.at(0, 16 * (NCH + 1)))
            for c in range(2):
                act.wait_ge(in_done[c], 16 * (NCH // 2 + 1))
                act.wait_ge(nb_done[c], 16 * (NCH // 2 + 1))

        @block.vector
        def _(dve):
            for s in (z_ready, u_ready, us_ready, prep_used, c_used, s_ready, cs_used, o_ready, dve_step,
                      h_done, y_used):
                dve.sem_inc(s.sem, s.per)
            z3, zq3 = heads(z[:]), heads(zq[:])

            def mul(o, x, y):
                return dve.tensor_tensor(o, x, y, ALU.mult)

            def add(o, x, y):
                return dve.tensor_tensor(o, x, y, ALU.add)

            def leaf_matrix(r, c, f):
                dve.wait_ge(prep_mm.sem, prep_mm.at(r, f + 1))
                if f == 0:
                    dve.wait_ge(decay_ready.sem, decay_ready.at(r, 1))
                cols = slice(COL[FILLS[f][0]], COL[FILLS[f][0]] + sum(NM * (LEAF - 1 - j) for j in FILLS[f]))
                mul(leafm[c][:, cols], leaf_bank[f % 2][:, 0:cols.stop - cols.start], decay[:, cols]
                    ).then_inc(prep_used.sem, 1)

            def masked(r, i, bank, parts):
                dve.wait_ge(prep_mm.sem, prep_mm.at(r, i))
                for dst, col, x, mask in parts:
                    ins = mul(dst.rearrange("p (x n) -> p x n", x=x),
                              bank[:, col:col + x * P].rearrange("p (x n) -> p x n", x=x),
                              mask.unsqueeze(1).broadcast_to([P, x, P]))
                ins.then_inc(prep_used.sem, 1)

            def grams8(r, c):
                masked(r, 5, bank_z[0], [(gram[c][:, 0:512], 0, 4, blk8)])

            def grams16(r, c):
                masked(r, 6, bank_p, [(gram[c][:, 512:1024], 0, 4, blk16)])

            def grams12(r, c):
                masked(r, 7, bank_p, [(grams[c][:, 0:256], 0, 2, ident), (grams[c][:, 256:512], 256, 2, blk2)])

            def grams4(r, c):
                masked(r, 8, bank_p, [(grams[c][:, 512:768], 0, 2, blk4)])

            def output(n, slot):
                unit = n + (NTB - 1) if slot < CARRY else n
                acc = yacc[:, bass.ds((unit % NTB) * (TB // P * HID) + slot % CARRY * HID, HID)]
                first = PAIRS * TT - TB // P if slot < CARRY else 0
                weight = dense[:, bass.ds(n * (TB // P) + (first + slot % CARRY), 1)]
                dve.wait_ge(y_mm.sem, y_mm.at(n, slot + 1))
                dve.scalar_tensor_tensor(out=acc, in0=bank_y[:, 0:HID], scalar=weight, in1=acc,
                                         op0=ALU.mult, op1=ALU.add).then_inc(y_used.sem, 1)

            for f in range(4):
                leaf_matrix(0, 0, f)
            grams8(0, 0)
            grams16(0, 0)
            grams12(0, 0)
            grams4(0, 0)
            with dve.Fori(0, PAIRS) as p, dve.Fori(0, NTB) as b:
                n = p * NTB + b
                for c in range(2):
                    m = n * 2 + c
                    r, rc = m + 1, 1 - c
                    marks = [0]

                    def mark(ins):
                        marks[0] += 1
                        ins.then_inc(dve_step.sem, 1)
                        return marks[0]

                    def need(k):
                        dve.wait_ge(dve_step.sem, dve_step.at(m, k))

                    def link(ins):
                        need(mark(ins))

                    def experts(slot):
                        if slot < FT:
                            dve.wait_ge(silu_done.sem, silu_done.at(n, slot + 1))
                            mul(htile(slot), htile(slot), bank_up[:]).then_inc(h_done.sem, 1)
                        output(n, slot)

                    def leaf(i):
                        for j in range(LEAF - 1):
                            k, t = LEAF - 1 - j, i * LEAF + j
                            part = tmp[:, 0:H * k].rearrange("p (h d) -> p h d", h=H)
                            link(mul(part, column(leafm[c], j).rearrange("p (h l) t -> p h l t", h=H)[:, :, i],
                                     z3[:, :, t:t + 1].broadcast_to([P, H, k])))
                            link(add(z3[:, :, t + 1:t + 1 + k], z3[:, :, t + 1:t + 1 + k], part))

                    dve.wait_ge(span_ready.sem, span_ready.at(m, 1))
                    v3 = heads(inb[c][:, 2 * HT:3 * HT])
                    p3 = heads(prec[:])
                    for x in range(2):
                        dve.wait_ge(z_mm.sem, z_mm.at(m, x + 1))
                        hs = slice(8 * x, 8 * x + 8)
                        zz = bank_z[x][:].rearrange("p (h x t) -> p h x t", h=8, x=2)
                        k1 = mark(mul(z3[:, hs], zz[:, :, 0], p3[:, hs]))
                        k2 = mark(mul(zq3[:, hs], zz[:, :, 1], p3[:, hs]))
                        need(k1)
                        dve.tensor_tensor(z3[:, hs], z3[:, hs], v3[:, hs], ALU.subtract).then_inc(z_ready.sem, 1)
                    dve.wait_ge(z_ready.sem, z_ready.at(m, 2))

                    def pair_level(i, width, t0):
                        g = width // 8
                        o = (t0 - 8) // 16 if width == 8 else 0
                        dve.wait_ge(c_mm.sem, c_mm.at(m, i))
                        cc = bank_c[:, 0:g * 256].rearrange("p (g x h t) -> p g x h t", g=g, x=2, t=width)
                        span = pre[width][c][:].rearrange("p (g h o t) -> p g h o t", g=g, o=16 // width,
                                                          t=width)[:, :, :, o]
                        zk = z3[:, :, t0:t0 + width].rearrange("p (g h) t -> p g h t", g=g)
                        zqk = zq3[:, :, t0:t0 + width].rearrange("p (g h) t -> p g h t", g=g)
                        tk = tmp[:, 0:H * width].rearrange("p (g h t) -> p g h t", g=g, t=width)
                        tq = tmpq[:, 0:H * width].rearrange("p (g h t) -> p g h t", g=g, t=width)
                        k1 = mark(mul(tk, cc[:, :, 0], span))
                        mul(tq, cc[:, :, 1], span).then_inc(c_used.sem, 1)
                        need(k1)
                        k2 = mark(add(zk, zk, tk))
                        dve.wait_ge(c_used.sem, c_used.at(m, i))
                        mark(add(zqk, zqk, tq))
                        need(k2)

                    dve.wait_ge(prep_used.sem, prep_used.at(m, 4))
                    leaf(0)
                    sp8 = [suf[8][c][:].rearrange("p (h o t) -> p h o t", h=H, o=2)[:, :, o] for o in range(2)]
                    mul(heads(u8[0]), z3[:, :, 0:8], sp8[0]).then_inc(u_ready.sem, 1)
                    experts(4 * c)
                    leaf_matrix(r, rc, 0)
                    pair_level(1, 8, 8)
                    leaf(1)
                    mul(heads(u16), z3[:, :, 0:16], heads(suf[16][c][:])).then_inc(u_ready.sem, 1)
                    experts(4 * c + 1)
                    leaf_matrix(r, rc, 1)
                    leaf_matrix(r, rc, 2)
                    pair_level(2, 16, 16)
                    leaf(2)
                    mul(heads(u8[1]), z3[:, :, 16:24], sp8[1]).then_inc(u_ready.sem, 1)
                    experts(4 * c + 2)
                    leaf_matrix(r, rc, 3)
                    pair_level(3, 8, 24)
                    leaf(3)
                    mul(uc[:], z[:], sufc[c][:]).then_inc(u_ready.sem, 1)
                    k = mark(mul(w[:], z[:], nb[c][:]))
                    grams8(r, rc)
                    need(k)
                    mul(blocks(us[:, 0:256], 2), halves(w[:], 2, 0), blocks(suf[2][c][:], 2))
                    mul(blocks(us[:, 256:512], 4), halves(w[:], 4, 0), blocks(suf[4][c][:], 4)
                        ).then_inc(us_ready.sem, 1)
                    experts(4 * c + 3)
                    grams16(r, rc)
                    for g in range(4):
                        dve.wait_ge(s_mm.sem, s_mm.at(m, g + 1))
                        for x in range(4):
                            h = 4 * g + x
                            own = st[:, h * D:(h + 1) * D]
                            ins = dve.scalar_tensor_tensor(out=own, in0=own, scalar=tot[c][:, h:h + 1],
                                                           in1=bank_z[g % 2][:, x * D:(x + 1) * D],
                                                           op0=ALU.mult, op1=ALU.add)
                        ins.then_inc(s_ready.sem, 1)
                    grams12(r, rc)
                    dve.wait_ge(cs_mm.sem, cs_mm.at(m, 1))
                    k1 = mark(add(halves(zq[:], 1, 1), halves(zq[:], 1, 1), blocks(bank_c[:, 0:256], 1)))
                    k2 = mark(mul(blocks(tmpq[:, 0:256], 2), blocks(bank_c[:, 256:512], 2),
                                  blocks(pre[2][c][:], 2)))
                    mul(blocks(tmpq[:, 256:512], 4), blocks(bank_gate[:, 0:256], 4), blocks(pre[4][c][:], 4)
                        ).then_inc(cs_used.sem, 1)
                    need(k2)
                    k2 = mark(add(halves(zq[:], 2, 1), halves(zq[:], 2, 1), blocks(tmpq[:, 0:256], 2)))
                    mark(mul(w[:], w[:], kq[c][:]))
                    need(k2)
                    link(add(halves(zq[:], 4, 1), halves(zq[:], 4, 1), blocks(tmpq[:, 256:512], 4)))
                    dve.wait_ge(o_out.sem, o_out.at(m, 16))
                    link(mul(ob[:], zq[:], a_cur[:]))
                    add(ob[:], ob[:], w[:]).then_inc(o_ready.sem, 1)
                    grams4(r, rc)
                    dve.wait_ge(o_ready.sem, o_ready.at(m, 1))
                    assert marks[0] == DVE_STEPS, marks[0]
            for slot in range(CARRY):
                output(PAIRS * NTB, slot)


def output_phase(nc, ps, spill, ospill, woT, yacc, lns, eps, centre, onesd, out):
    with ExitStack() as ctx:
        def sb(name, n):
            return ctx.enter_context(nc.sbuf_tensor(name, [P, n], F32))

        def counted(name, per, first=None):
            return Counted(ctx.enter_context(nc.semaphore(name)), per, first)

        def two(name, n):
            return [sb(f"{name}{x}", n) for x in range(2)]

        wo = sb("wo", H * HID)
        o = two("o", CPB * HT)
        g = two("g", CPB * HT)
        og = two("og", CPB * HT)
        sq = sb("osq", CPB * HT)
        rs = sb("ors", CPB * HT)
        on = two("on", HT)
        wo_in = ctx.enter_context(nc.semaphore("wo_in"))
        o_in = [ctx.enter_context(nc.semaphore(f"o_in{x}")) for x in range(2)]
        g_in = [ctx.enter_context(nc.semaphore(f"g_in{x}")) for x in range(2)]
        centre_mm = counted("o_centre_mm", CPB)
        squared = counted("o_squared", CPB)
        var_mm = counted("o_var_mm", CPB)
        logged = counted("o_logged", CPB)
        rs_ready = counted("o_rs", CPB)
        normed = counted("o_normed", CPB)
        gated = counted("o_gated", CPB)
        proj_mm = counted("o_proj_mm", 1, 2)
        y_ready = counted("y_ready", 1, 2)
        y_out = ctx.enter_context(nc.semaphore("y_out"))
        block = ctx.enter_context(nc.Block())
        bank_centre, bank_var, bank_proj = ps[0:4], ps[4:6], ps[6:8]

        def part(t, c):
            return t[:, c * HT:(c + 1) * HT]

        def tiles(engine, step):
            step(0, 0)
            with engine.Fori(0, TT // 2 - 2) as n:
                step(n * 2 + 1, 1)
                step(n * 2 + 2, 0)
            step(TT - 3, 1)
            step(TT - 2, 0)
            step(TT - 1, 1)

        @block.sync
        def _(sp):
            def load_o(x, t):
                sp.dma_start(o[x][:].rearrange("p (c n) -> p c n", c=CPB),
                             ospill[bass.ds(t * CPB + 1, CPB)].rearrange("c p n -> p c n")).then_inc(o_in[x], 16)

            def load_g(x, t):
                sp.dma_start(g[x][:].rearrange("p (c n) -> p c n", c=CPB),
                             spill[bass.ds(t * CPB + CPB, CPB), :, G_ * HT:NT * HT].rearrange("c p n -> p c n")
                             ).then_inc(g_in[x], 16)

            def store(t):
                sp.wait_ge(y_ready.sem, y_ready.at(t, 1))
                sp.dma_start(out[bass.ds(t, 1)].rearrange("o p c -> p (o c)"),
                             yacc[:, bass.ds(t * HID, HID)]).then_inc(y_out, 16)

            def step(t, x):
                if not (isinstance(t, int) and t >= TT - 2):
                    sp.wait_ge(centre_mm.sem, centre_mm.at(t, CPB))
                    load_o(x, t + 2)
                    sp.wait_ge(gated.sem, gated.at(t, CPB))
                    load_g(x, t + 2)
                if not (isinstance(t, int) and t == 0):
                    store(t - 1)

            load_o(0, 0)
            sp.dma_start(wo[:], woT).then_inc(wo_in, 16)
            load_g(0, 0)
            load_o(1, 1)
            load_g(1, 1)
            tiles(sp, step)
            store(TT - 1)
            sp.wait_ge(y_out, 16 * TT)

        @block.tensor
        def _(pe):
            for s in (centre_mm, var_mm, proj_mm):
                pe.sem_inc(s.sem, s.first)

            def centred(t, c, x):
                pe.wait_ge(normed.sem, normed.at(t, c + 1 - CPB))
                pe.matmul(bank_centre[c][:], centre, part(o[x], c), start=True, stop=True
                          ).then_inc(centre_mm.sem, 1)

            def variance(t, c):
                pe.wait_ge(squared.sem, squared.at(t, c + 1))
                pe.wait_ge(logged.sem, logged.at(t, c - 1))
                pe.matmul(bank_var[c % 2][:], onesd[:], part(sq, c), start=True, stop=True
                          ).then_inc(var_mm.sem, 1)

            def project(t, x):
                pe.wait_ge(gated.sem, gated.at(t, CPB))
                pe.wait_ge(y_ready.sem, y_ready.at(t, -1))
                for h in range(H):
                    mm = pe.matmul(bank_proj[x][:, 0:HID], og[x][:, h * P:(h + 1) * P],
                                   wo[:, h * HID:(h + 1) * HID], start=(h == 0), stop=(h == H - 1))
                mm.then_inc(proj_mm.sem, 1)

            def step(t, x):
                first = isinstance(t, int) and t == 0
                pe.wait_ge(o_in[x], (t - x) * 8 + 16)
                for c in range(CPB):
                    centred(t, c, x)
                    if c:
                        variance(t, c - 1)
                variance(t, CPB - 1)
                if not first:
                    project(t - 1, 1 - x)

            pe.wait_ge(wo_in, 16)
            tiles(pe, step)
            project(TT - 1, 1)

        @block.scalar
        def _(act):
            for s in (squared, logged, rs_ready):
                act.sem_inc(s.sem, s.per)

            def square(t, c):
                act.wait_ge(centre_mm.sem, centre_mm.at(t, c + 1))
                act.wait_ge(var_mm.sem, var_mm.at(t, c + 1 - CPB))
                act.activation(part(sq, c), bank_centre[c][:], ACT.Square).then_inc(squared.sem, 1)

            def step(t, x):
                square(t, 0)
                for c in range(CPB):
                    if c + 1 < CPB:
                        square(t, c + 1)
                    act.wait_ge(var_mm.sem, var_mm.at(t, c + 1))
                    act.wait_ge(normed.sem, normed.at(t, c + 1 - CPB))
                    act.activation(part(rs, c), bank_var[c % 2][:], ACT.Ln, bias=eps[:, 0:1]
                                   ).then_inc(logged.sem, 1)
                for c in range(CPB):
                    act.wait_ge(logged.sem, logged.at(t, c + 1))
                    act.activation(part(rs, c), part(rs, c), ACT.Exp, scale=-0.5).then_inc(rs_ready.sem, 1)

            tiles(act, step)

        @block.vector
        def _(dve):
            for s in (normed, gated, y_ready):
                dve.sem_inc(s.sem, s.first)

            def add(t, x):
                dve.wait_ge(proj_mm.sem, proj_mm.at(t, 1))
                acc = yacc[:, bass.ds(t * HID, HID)]
                dve.tensor_tensor(acc, acc, bank_proj[x][:, 0:HID], ALU.add).then_inc(y_ready.sem, 1)

            def step(t, x):
                for c in range(CPB):
                    y = c % 2
                    dve.wait_ge(rs_ready.sem, rs_ready.at(t, c + 1))
                    dve.scalar_tensor_tensor(out=on[y][:], in0=bank_centre[c][:], scalar=lns[:, 0:1],
                                             in1=part(rs, c), op0=ALU.mult, op1=ALU.mult
                                             ).then_inc(normed.sem, 1)
                    if c == 0:
                        dve.wait_ge(g_in[x], (t - x) * 8 + 16)
                        dve.wait_ge(proj_mm.sem, proj_mm.at(t, -1))
                    dve.wait_ge(normed.sem, normed.at(t, c + 1))
                    dve.scalar_tensor_tensor(out=og[x][:].rearrange("p (h c t) -> p c h t", h=H, c=CPB)[:, c],
                                             in0=heads(on[y][:]), scalar=lns[:, 1:2],
                                             in1=heads(part(g[x], c)), op0=ALU.add, op1=ALU.mult
                                             ).then_inc(gated.sem, 1)
                if not (isinstance(t, int) and t == 0):
                    add(t - 1, 1 - x)

            tiles(dve, step)
            add(TT - 1, 1)


_OUT = "y_out_dram"


def kernel(**inputs):
    import numpy as np
    import concourse.bacc as bacc
    from concourse.bass_utils import run_bass_kernel_spmd

    def get(name):
        return np.asarray(inputs["L0_" + name])

    def columns(w):
        n = w.shape[0]
        return w.T.reshape(KT, P, n).transpose(1, 0, 2).reshape(P, KT * n)

    def per_head(v):
        return v.reshape(H, D).T

    def expert_columns(w):
        t = w.reshape(PAIRS, FT, P, KT, P)
        return t.transpose(0, 4, 1, 3, 2).reshape(PAIRS, P, FT * KT * P)

    x = get("attn_x").reshape(S, HID)
    taps = np.stack([get(f"attn_{n}c_w").reshape(H, D, TAPS) for n in "kqv"])
    e = np.arange(P)
    masks = [(e[:, None] // m == e[None, :] // m) for m in (1, 2, 4, 8, 16)]
    ties = np.tile((np.arange(E)[None, :] < np.arange(8)[:, None]).reshape(1, P), (P, 1))
    arrays = {
        "x": x,
        "xT": columns(x),
        "projT": np.stack([columns(get(f"attn_W{n}")) for n in "kqvag"]),
        "wbT": columns(get("attn_Wb")),
        "gateT": columns(get("ffn_gate_inp")),
        "convw": taps.transpose(2, 0, 1, 3).reshape(P, 3 * H * TAPS),
        "chan": np.concatenate([per_head(get(n)) for n in ("attn_kc_b", "attn_qc_b", "attn_vc_b", "attn_ba")], 1),
        "bb": get("attn_bb").reshape(H, 1),
        "lnp": np.stack([get("attn_ln_g"), get("attn_ln_b")], 1),
        "woT": get("attn_Wo").T.reshape(H, D, HID).transpose(1, 0, 2).reshape(D, H * HID),
        "wupT": expert_columns(get("ffn_W_up")),
        "wgT": expert_columns(get("ffn_W_gate")),
        "wdT": get("ffn_W_down").transpose(0, 2, 1).reshape(PAIRS, FT, P, HID).transpose(0, 2, 1, 3)
               .reshape(PAIRS, P, FT * HID),
        "consts": np.concatenate([*masks, ties], 1).astype(np.float32),
    }
    arrays = {n: np.ascontiguousarray(a) for n, a in arrays.items()}
    nc = bacc.Bacc("TRN2", target_bir_lowering=False, num_devices=1)
    args = [nc.dram_tensor(f"{n}_dram", a.shape, F32, kind="ExternalInput").ap() for n, a in arrays.items()]
    out = nc.dram_tensor(_OUT, (TT, P, HID), F32, kind="ExternalOutput").ap()
    build(nc, *args, out)
    r = run_bass_kernel_spmd(nc, [{f"{n}_dram": a for n, a in arrays.items()}], core_ids=[0])
    return r.results[0][_OUT].reshape(1, S, HID)
```

```python
from contextlib import ExitStack

import concourse.bass as bass
from concourse import mybir

F32 = mybir.dt.float32
ALU = mybir.AluOpType
ACT = mybir.ActivationFunctionType
AX = mybir.AxisListType

P = 128
S = 2048
HID = 256
KT = HID // P
H = 16
D = 128
TAPS = 4
HALO = TAPS - 1
SCALE = float(D) ** -0.5
EPS = 1e-5
E = 16
TOPK = 4
F = 448
PAIRS = E // 2
FT = 2 * F // P
FH = F - 3 * P
TB = 512
NTB = S // TB
CH = 32
NCH = S // CH
LEAF = 8
NLEAF = CH // LEAF
HT = H * CH
NM = H * NLEAF
TT = S // P
CPB = P // CH
BLK = 256
CPP = BLK // CH
HH = H // 2
NR = 2 * S // BLK
FRONT = CPP
K_, Q_, V_, A_, G_ = range(5)
NT = 5
POOL_STEPS = 15
DVE_STEPS = 74


class Counted:

    def __init__(self, sem, per, first=None):
        self.sem, self.per, self.first = sem, per, first or per

    def at(self, r, j):
        return r * self.per + (self.first + j)


def heads(ap, n=H):
    return ap.rearrange("p (h t) -> p h t", h=n)


def build(nc, x, xT, projT, wbT, gateT, convw, chan, bb, lnp, woT, wupT, wgT, wdT, consts, out):
    spill = nc.dram_tensor("spill", (FRONT + NCH + 2, P, NT * HT), F32, kind="Internal").ap()
    betas = nc.dram_tensor("betas", (NCH + 2, 1, HT), F32, kind="Internal").ap()
    ospill = nc.dram_tensor("ospill", (NCH + 1, P, HT), F32, kind="Internal").ap()
    with ExitStack() as ctx:
        def sb(name, n, parts=P, c=ctx):
            return c.enter_context(nc.sbuf_tensor(name, [parts, n], F32))

        ps = [ctx.enter_context(nc.psum_tensor(f"bank{i}", [P, 512], F32)) for i in range(8)]
        xn = sb("xn", KT * (HALO + S))
        xn3 = xn[:].rearrange("p (k t) -> p k t", k=KT)
        yacc = sb("yacc", TT * HID)
        cst = sb("cst", 6 * P)
        ident, blk2, blk4, blk8, blk16 = (cst[:, i * P:(i + 1) * P] for i in range(5))
        ties = cst[:, 5 * P:6 * P]
        dense = sb("dense", TT * E)
        chs = sb("chs", 4 * H)
        cw = sb("cw", 3 * H * TAPS)
        lns = sb("lns", 2)
        bbs = sb("bbs", 1, H)
        eps = sb("eps", 1)
        ones = sb("ones", P)
        onesh = sb("onesh", P)
        onesd = sb("onesd", P)
        centre = ties

        with ExitStack() as early:
            w = [sb(f"w{i}", KT * H * D, c=early) for i in range(NT)]
            w_in = [early.enter_context(nc.semaphore(f"w_in{i}")) for i in range(NT)]
            norm_phase(nc, ps, x, xT, wbT, gateT, convw, chan, bb, lnp, consts, betas, xn, yacc, cst, dense, chs,
                       cw, lns, bbs, eps, ones, onesh, onesd, ties, projT, w, w_in)
            projection_phase(nc, ps, spill, xn3, chs, cw, w, w_in)
        recurrence_phase(nc, ps, spill, ospill, betas, wupT, wgT, wdT, xn3, yacc, ident, blk2, blk4, blk8, blk16,
                         dense, ones,
                         onesd, ties)
        output_phase(nc, ps, spill, ospill, woT, yacc, lns, eps, centre, onesd, out)


def norm_phase(nc, ps, x, xT, wbT, gateT, convw, chan, bb, lnp, consts, betas, xn, yacc, cst, dense, chs,
               cw, lns, bbs, eps, ones, onesh, onesd, ties, projT, w, w_in):
    xn3 = xn[:].rearrange("p (k t) -> p k t", k=KT)
    NB4 = S // 512
    with ExitStack() as ctx:
        def sb(name, n, parts=P):
            return ctx.enter_context(nc.sbuf_tensor(name, [parts, n], F32))

        def sem(name):
            return ctx.enter_context(nc.semaphore(name))

        xr = sb("xr", KT * S)
        xr3 = xr[:].rearrange("p (k t) -> p k t", k=KT)
        sq = sb("sq", KT * S)
        sq3 = sq[:].rearrange("p (k t) -> p k t", k=KT)
        inv = sb("inv", S)
        nbh = sb("nbh", S + 2 * CH, H)
        wb = sb("wb", KT * H)
        gt = sb("gt", KT * E)
        x_in = sem("x_in")
        small_in = sem("small_in")
        made = sem("made")
        mean_done = sem("mean_done")
        centred = sem("centred")
        squared = sem("squared")
        var_done = sem("var_done")
        logged = sem("logged")
        inv_done = sem("inv_done")
        normed = sem("normed")
        beta_mm = sem("beta_mm")
        beta_sig = sem("beta_sig")
        negated = sem("negated")
        beta_out = sem("beta_out")
        logits_mm = sem("logits_mm")
        block = ctx.enter_context(nc.Block())

        @block.sync
        def _(sp):
            sp.dma_start(xr[:], xT).then_inc(x_in, 16)
            loads = [(cst[:], consts), (wb[:], wbT), (gt[:], gateT), (cw[:], convw), (chs[:], chan),
                     (bbs[:], bb), (lns[:], lnp),
                     (yacc[:].rearrange("p (n c) -> p n c", n=TT), x.rearrange("(n p) c -> p n c", p=P))]
            for dst, src in loads:
                sp.dma_start(dst, src).then_inc(small_in, 16)
            for i in range(NT):
                sp.dma_start(w[i][:], projT[i]).then_inc(w_in[i], 16)
            sp.wait_ge(small_in, 16 * len(loads))
            sp.wait_ge(made, 1)
            sp.wait_ge(negated, NB4)
            sp.dma_start(betas.rearrange("c o (h t) -> h (o c) t", h=H),
                         nbh[:].rearrange("h (c t) -> h c t", t=CH)).then_inc(beta_out, 16)
            sp.wait_ge(beta_out, 16)

        @block.gpsimd
        def _(pool):
            pool.memset(ones[:], 1.0)
            pool.memset(onesh[:], 1.0 / HID)
            pool.memset(onesd[:], 1.0 / D)
            pool.memset(eps[:], EPS)
            pool.memset(nbh[:, S:S + 2 * CH], 0.0)
            pool.memset(xn3[:, :, 0:HALO], 0.0).then_inc(made, 1)

        @block.tensor
        def _(pe):
            pe.wait_ge(made, 1)
            pe.wait_ge(x_in, 16)
            for b in range(NB4):
                for k in range(KT):
                    mm = pe.matmul(ps[b][:], onesh[:], xr3[:, k, b * 512:(b + 1) * 512],
                                   start=(k == 0), stop=(k == KT - 1))
                mm.then_inc(mean_done, 1)
            for b in range(NB4):
                pe.wait_ge(squared, b + 1)
                for k in range(KT):
                    mm = pe.matmul(ps[4 + b][:], onesh[:], sq3[:, k, b * 512:(b + 1) * 512],
                                   start=(k == 0), stop=(k == KT - 1))
                mm.then_inc(var_done, 1)
            pe.wait_ge(small_in, 16 * 8)
            for b in range(NB4):
                pe.wait_ge(normed, KT * (b + 1))
                for k in range(KT):
                    mm = pe.matmul(ps[b][0:H, :], wb[:, k * H:(k + 1) * H],
                                   xn3[:, k, HALO + b * 512:HALO + (b + 1) * 512],
                                   start=(k == 0), stop=(k == KT - 1))
                mm.then_inc(beta_mm, 1)
            for t in range(TT):
                for k in range(KT):
                    mm = pe.matmul(ps[4][:, t * E:(t + 1) * E], xn3[:, k, HALO + t * P:HALO + (t + 1) * P],
                                   gt[:, k * E:(k + 1) * E], start=(k == 0), stop=(k == KT - 1))
            mm.then_inc(logits_mm, 1)

        @block.scalar
        def _(act):
            for b in range(NB4):
                act.wait_ge(centred, KT * (b + 1))
                act.activation(sq3[:, :, b * 512:(b + 1) * 512], xr3[:, :, b * 512:(b + 1) * 512],
                               ACT.Square).then_inc(squared, 1)
            for b in range(NB4):
                act.wait_ge(var_done, b + 1)
                act.activation(inv[:, b * 512:(b + 1) * 512], ps[4 + b][:], ACT.Ln,
                               bias=eps[:, 0:1]).then_inc(logged, 1)
            for b in range(NB4):
                act.wait_ge(logged, b + 1)
                blk = inv[:, b * 512:(b + 1) * 512]
                act.activation(blk, blk, ACT.Exp, scale=-0.5).then_inc(inv_done, 1)
            for b in range(NB4):
                act.wait_ge(beta_mm, b + 1)
                act.activation(nbh[:, b * 512:(b + 1) * 512], ps[b][0:H, :], ACT.Sigmoid,
                               bias=bbs[:, 0:1]).then_inc(beta_sig, 1)

        @block.vector
        def _(dve):
            for b in range(NB4):
                dve.wait_ge(mean_done, b + 1)
                for k in range(KT):
                    blk = xr3[:, k, b * 512:(b + 1) * 512]
                    dve.tensor_tensor(blk, blk, ps[b][:], ALU.subtract).then_inc(centred, 1)
            for b in range(NB4):
                blk = inv[:, b * 512:(b + 1) * 512]
                dve.wait_ge(inv_done, b + 1)
                for k in range(KT):
                    dve.tensor_tensor(xn3[:, k, HALO + b * 512:HALO + (b + 1) * 512],
                                      xr3[:, k, b * 512:(b + 1) * 512], blk, ALU.mult).then_inc(normed, 1)
            for b in range(NB4):
                blk = nbh[:, b * 512:(b + 1) * 512]
                dve.wait_ge(beta_sig, b + 1)
                dve.tensor_scalar(blk, blk, -1.0, None, ALU.mult).then_inc(negated, 1)
            dve.wait_ge(logits_mm, 1)
            dve.tensor_copy(dense[:], ps[4][:, 0:TT * E])


def projection_phase(nc, ps, spill, xn3, chs, cw, w, w_in):
    with ExitStack() as ctx:
        def sb(name, n):
            return ctx.enter_context(nc.sbuf_tensor(name, [P, n], F32))

        def counted(name, per):
            return Counted(ctx.enter_context(nc.semaphore(name)), per)

        w3 = [t[:].rearrange("p (k n) -> p k n", k=KT) for t in w]
        st = [sb(f"st{x}", CPP * NT * HH * CH) for x in range(2)]
        st_half = CPP * NT * HH * CH // 2
        st4 = [t[:].rearrange("p (c x h t) -> p c x h t", c=CPP, x=NT, h=HH) for t in st]
        sg = [sb(f"sg{x}", 3 * BLK) for x in range(2)]
        sg3 = [t[:].rearrange("p (c x t) -> p c x t", c=CPP, x=3) for t in sg]
        scale = sb("scale", 1)
        cleared = ctx.enter_context(nc.semaphore("st_cleared"))
        padded = ctx.enter_context(nc.semaphore("padded"))
        taps_mm = counted("taps_mm", HH)
        gates_mm = counted("gates_mm", HH)
        tap3_done = counted("tap3_done", 3 * HH)
        gates_done = counted("gates_done", 2 * HH)
        conv_done = counted("conv_done", 3 * HH)
        conv_step = counted("conv_step", 6 * HH)
        sig_done = counted("sig_done", HH)
        silu_done = counted("silu_done", HH)
        finished = counted("finished", HH)
        out_done = counted("proj_out", 16 * CPP)
        block = ctx.enter_context(nc.Block())
        taps_ps = [[ps[4 * x + i][:, 0:HALO + BLK] for i in range(3)] for x in range(2)]
        gates_ps = [ps[4 * x + 3][:].rearrange("p (x t) -> p x t", x=2) for x in range(2)]

        def rounds(engine, step):
            with engine.Fori(0, NR // 2) as b:
                for x in range(2):
                    step(b, b * 2 + x, x)

        @block.sync
        def _(sp):
            sp.sem_inc(out_done.sem, out_done.per)

            def store(b, r, x):
                sp.wait_ge(gates_done.sem, gates_done.at(r, 0))
                sp.wait_ge(finished.sem, finished.at(r, 1))
                for c in range(CPP):
                    row = spill[bass.ds(b * CPP + (c + (FRONT if x else 0)), 1)]
                    sp.dma_start(row.rearrange("c p (x y n) -> p (c x) y n", x=NT, y=2)[:, :, 1 - x],
                                 st[1 - x][:].rearrange("p (c x n) -> p c x n", c=CPP, x=NT)[:, c]
                                 ).then_inc(out_done.sem, 16)

            sp.wait_ge(cleared, 2)
            for c in range(2):
                sp.dma_start(spill[FRONT + NCH + c], st[1][:, 0:NT * HT]).then_inc(padded, 16)
            rounds(sp, store)
            store(NR // 2, NR, 0)
            sp.wait_ge(padded, 32)
            sp.wait_ge(out_done.sem, out_done.at(NR + 1, 0))

        @block.tensor
        def _(pe):
            pe.sem_inc(taps_mm.sem, taps_mm.per)
            pe.sem_inc(gates_mm.sem, gates_mm.per)
            for i in range(NT):
                pe.wait_ge(w_in[i], 16)

            def project(b, r, x):
                for h in range(HH):
                    cols = slice((x * HH + h) * D, (x * HH + h + 1) * D)
                    pe.wait_ge(conv_done.sem, conv_done.at(r, 3 * (h - 1)))
                    for i in (K_, Q_, V_):
                        for k in range(KT):
                            mm = pe.matmul(taps_ps[h % 2][i], w3[i][:, k, cols],
                                           xn3[:, k, bass.ds(b * BLK, HALO + BLK)],
                                           start=(k == 0), stop=(k == KT - 1))
                    mm.then_inc(taps_mm.sem, 1)
                    pe.wait_ge(gates_done.sem, gates_done.at(r, 2 * (h - 1)))
                    for i in (A_, G_):
                        for k in range(KT):
                            mm = pe.matmul(gates_ps[h % 2][:, i - A_], w3[i][:, k, cols],
                                           xn3[:, k, bass.ds(b * BLK + HALO, BLK)],
                                           start=(k == 0), stop=(k == KT - 1))
                    mm.then_inc(gates_mm.sem, 1)

            rounds(pe, project)

        @block.scalar
        def _(act):
            for s in (tap3_done, gates_done, sig_done):
                act.sem_inc(s.sem, s.per)
            act.wait_ge(cleared, 2)

            def sigmoid(r, j, y, h):
                act.wait_ge(conv_done.sem, conv_done.at(r, 3 * j))
                act.wait_ge(silu_done.sem, silu_done.at(r, j - 1))
                act.activation(sg3[h % 2], st4[y][:, :, 0:3, h], ACT.Sigmoid).then_inc(sig_done.sem, 1)

            def head(b, r, x):
                act.wait_ge(out_done.sem, out_done.at(r, 0))
                if x:
                    act.wait_ge(padded, 32)
                for h in range(HH):
                    g = x * HH + h
                    act.wait_ge(taps_mm.sem, taps_mm.at(r, h + 1))
                    for i in (K_, Q_, V_):
                        act.activation(st4[x][:, :, i, h], taps_ps[h % 2][i][:, HALO:].rearrange(
                            "p (c t) -> p c t", c=CPP), ACT.Identity, bias=chs[:, i * H + g:i * H + g + 1],
                            scale=cw[:, (i * H + g) * TAPS + HALO:(i * H + g) * TAPS + TAPS]
                        ).then_inc(tap3_done.sem, 1)
                    act.wait_ge(gates_mm.sem, gates_mm.at(r, h + 1))
                    act.activation(st4[x][:, :, A_, h], gates_ps[h % 2][:, 0].rearrange(
                        "p (c t) -> p c t", c=CPP), ACT.Sigmoid, bias=chs[:, 3 * H + g:3 * H + g + 1]
                    ).then_inc(gates_done.sem, 1)
                    act.activation(st4[x][:, :, G_, h], gates_ps[h % 2][:, 1].rearrange(
                        "p (c t) -> p c t", c=CPP), ACT.Sigmoid).then_inc(gates_done.sem, 1)
                    if h == 0:
                        sigmoid(r, 0, 1 - x, HH - 1)
                    else:
                        sigmoid(r, h, x, h - 1)

            rounds(act, head)
            sigmoid(NR, 0, 1, HH - 1)

        @block.vector
        def _(dve):
            dve.sem_inc(conv_done.sem, conv_done.per)
            dve.sem_inc(conv_step.sem, conv_step.per)
            dve.memset(st[1][:, st_half:], 0.0).then_inc(cleared, 1)

            def convolve(b, r, x):
                for h in range(HH):
                    dve.wait_ge(tap3_done.sem, tap3_done.at(r, 3 * h + 3))
                    for tap in (2, 1, 0):
                        for i in (K_, Q_, V_):
                            acc = st4[x][:, :, i, h]
                            if tap < 2:
                                dve.wait_ge(conv_step.sem, conv_step.at(r, 6 * h + 3 * (1 - tap) + i + 1))
                            w0 = (i * H + x * HH + h) * TAPS + tap
                            ins = dve.scalar_tensor_tensor(
                                out=acc, in0=taps_ps[h % 2][i][:, tap:tap + BLK].rearrange(
                                    "p (c t) -> p c t", c=CPP),
                                scalar=cw[:, w0:w0 + 1], in1=acc, op0=ALU.mult, op1=ALU.add)
                            ins.then_inc(conv_step.sem if tap else conv_done.sem, 1)

            rounds(dve, convolve)

        @block.gpsimd
        def _(pool):
            pool.sem_inc(finished.sem, finished.per)
            pool.sem_inc(silu_done.sem, silu_done.per)
            pool.memset(st[1][:, 0:st_half], 0.0)
            pool.memset(scale[:], SCALE).then_inc(cleared, 1)
            pool.wait_ge(cleared, 2)
            pool.wait_ge(padded, 32)

            def finish(r, j, y, h):
                pool.wait_ge(sig_done.sem, sig_done.at(r, j + 1))
                kqv = st4[y][:, :, 0:3, h]
                pool.tensor_tensor(kqv, kqv, sg3[h % 2], ALU.mult).then_inc(silu_done.sem, 1)
                pool.wait_ge(silu_done.sem, silu_done.at(r, j + 1))
                k = st4[y][:, :, K_, h]
                pool.tensor_tensor(k, k, scale[:].unsqueeze(2).broadcast_to([P, CPP, CH]), ALU.mult
                                   ).then_inc(finished.sem, 1)

            def step(b, r, x):
                finish(r, 0, 1 - x, HH - 1)
                for j in range(1, HH):
                    finish(r, j, x, j - 1)

            rounds(pool, step)
            finish(NR, 0, 1, HH - 1)


def recurrence_phase(nc, ps, spill, ospill, betas, wupT, wgT, wdT, xn3, yacc, ident, blk2, blk4, blk8, blk16, dense,
                     ones, onesd, ties):
    bank_z = ps[0:2]
    bank_t, bank_c, bank_p = ps[2], ps[3], ps[4]
    bank_gate, bank_up, bank_y = ps[5], ps[6], ps[7]
    leaf_bank = (bank_p, bank_z[0])
    FILLS = [(0, 6), (1, 5), (2, 4), (3,)]
    COL, LM = {}, 0
    for js in FILLS:
        for j in js:
            COL[j] = LM
            LM += NM * (LEAF - 1 - j)

    def column(ap, j, base=0):
        n = LEAF - 1 - j
        return ap[:, COL[j] - base:COL[j] - base + NM * n].rearrange("p (m t) -> p m t", t=n)

    CARRY = 3
    OUTPUTS = [(1, 1), (1, 2), (1, 3), (0, 0), (0, 1), (0, 2), (0, 3), (1, 0)]
    SLOT_OUTPUTS = [(0,), (1,), (2,), (), (3,), (4,), (5,), (6, 7)]
    SLOTS = len(OUTPUTS)
    output_bank = [bank_y] * 7 + [bank_gate]

    with ExitStack() as ctx:
        def sb(name, n, parts=P):
            return ctx.enter_context(nc.sbuf_tensor(name, [parts, n], F32))

        def counted(name, per):
            return Counted(ctx.enter_context(nc.semaphore(name)), per)

        def two(name, n):
            return [sb(f"{name}{c}", n) for c in range(2)]

        inb = two("inb", 4 * HT)
        leafm = two("leafm", LM)
        decay = sb("decay", LM)
        nb = two("nb", HT)
        pre = {m: two(f"pre{m}_", HT // 2) for m in (2, 4, 8, 16)}
        suf = {m: two(f"suf{m}_", HT // 2) for m in (2, 4, 8, 16)}
        prec = sb("prec", HT)
        sufc = two("sufc", HT)
        tot = two("tot", H)
        kc = {m: sb(f"kc{m}_", HT // 2) for m in (2, 4, 8, 16)}
        gram = two("gram", 4 * 2 * P)
        grams = two("grams", 6 * P)
        kq = two("kq", HT)
        prod = two("prod", 512)
        runa = {m: sb(f"runa{m}", H * CH // m) for m in (2, 4, 8, 16)}
        runs = sb("runs", HT)
        z = sb("z", HT)
        zq = sb("zq", HT)
        w = z
        tmp = sb("tmp", HT)
        tmpq = sb("tmpq", HT)
        uc = sb("uc", HT)
        u8 = [uc[:, 0:H * 8], uc[:, H * 8:H * 16]]
        u16 = uc[:, H * 16:H * 32]
        us = tmpq
        uts = sb("uts", 6 * P)
        ut = uts[:, 0:2 * P]
        utc = tmp
        a_cur = sb("a_cur", HT)
        kn = sb("kn", 4 * 512)
        kn4 = kn[:].rearrange("p (g h d) -> p g h d", g=4, h=4)
        st = sb("state", H * D)
        stT = sb("stateT", H * D)
        ob = sb("ob", HT)
        wu = sb("wu", FT * KT * P)
        wg = sb("wg", FT * KT * P)
        wd = sb("wd", FT * HID)
        hT = sb("hT", FT * TB)

        in_done = [ctx.enter_context(nc.semaphore(f"in_done{c}")) for c in range(2)]
        nb_done = [ctx.enter_context(nc.semaphore(f"nb_done{c}")) for c in range(2)]
        o_out = counted("o_out", 16)
        z_mm = counted("z_mm", 2)
        ktr_mm = counted("ktr_mm", 1)
        prep_mm = counted("prep_mm", 8)
        kq_mm = counted("kq_mm", 1)
        ut_mm = counted("ut_mm", 4)
        c_mm = counted("c_mm", 3)
        s_mm = counted("s_mm", 4)
        st_mm = counted("st_mm", 4)
        uts_mm = counted("uts_mm", 1)
        cs_mm = counted("cs_mm", 1)
        kn_cp = counted("kn_cp", 4)
        a_cp = counted("a_cp", 1)
        kc_cp = counted("kc_cp", 1)
        kq_cp = counted("kq_cp", 1)
        ut_cp = counted("ut_cp", 4)
        st_cp = counted("st_cp", 4)
        uts_cp = counted("uts_cp", 1)
        z_ready = counted("z_ready", 2)
        u_ready = counted("u_ready", 4)
        w_ready = counted("w_ready", 1)
        us_ready = counted("us_ready", 1)
        wk_ready = counted("wk_ready", 1)
        st_scaled = counted("st_scaled", 4)
        prep_used = counted("prep_used", 8)
        c_used = counted("c_used", 3)
        s_ready = counted("s_ready", 4)
        cs_used = counted("cs_used", 1)
        o_ready = counted("o_ready", 1)
        dve_step = counted("dve_step", DVE_STEPS)
        prod_ready = counted("prod_ready", 5)
        decay_ready = counted("decay_ready", 1)
        span_ready = counted("span_ready", 1)
        pool_step = counted("pool_step", POOL_STEPS)
        ffn_mm = counted("ffn_mm", FT)
        silu_done = counted("silu_done", FT)
        h_done = counted("h_done", FT)
        y_mm = counted("y_mm", SLOTS)
        y_used = counted("y_used", SLOTS)
        wgu_in = [ctx.enter_context(nc.semaphore(f"wgu_in{i}")) for i in range(FT)]
        wd_in = [ctx.enter_context(nc.semaphore(f"wd_in{i}")) for i in range(2)]
        cleared = ctx.enter_context(nc.semaphore("cleared"))
        route_step = ctx.enter_context(nc.semaphore("route_step"))
        shift_done = ctx.enter_context(nc.semaphore("shift_done"))
        exp_done = ctx.enter_context(nc.semaphore("exp_done"))
        table_in = ctx.enter_context(nc.semaphore("table_in"))
        block = ctx.enter_context(nc.Block())

        shifted, exps, rank, chosen, share = (stT[:, i * 256:(i + 1) * 256] for i in range(5))
        top, total = stT[:, 1280:1280 + TT], stT[:, 1280 + TT:1280 + 2 * TT]
        cmp_gt, cmp_eq = st[:, 0:4 * E * E], st[:, 4 * E * E:8 * E * E]

        def routing(dve, leaf_matrix):
            n = [0]

            def link(ins):
                n[0] += 1
                ins.then_inc(route_step, 1)
                dve.wait_ge(route_step, n[0])

            def by_token(ap):
                return ap.rearrange("p (t e) -> p t e", t=TT)

            link(dve.tensor_reduce(top, by_token(dense[:]), AX.X, ALU.max))
            dve.tensor_tensor(by_token(shifted), by_token(dense[:]),
                              top.unsqueeze(2).broadcast_to([P, TT, E]), ALU.subtract).then_inc(shift_done, 1)
            tie = ties.rearrange("p (e f) -> p e f", e=8)
            g4 = cmp_gt.rearrange("p (t e f) -> p t e f", t=4, e=E)
            q4 = cmp_eq.rearrange("p (t e f) -> p t e f", t=4, e=E)
            for t0 in range(0, TT, 4):
                for u in range(4):
                    row = dense[:, (t0 + u) * E:(t0 + u + 1) * E]
                    other = row.unsqueeze(1).broadcast_to([P, E, E])
                    own = row.unsqueeze(2).broadcast_to([P, E, E])
                    dve.tensor_tensor(g4[:, u], other, own, ALU.is_gt)
                    link(dve.tensor_tensor(q4[:, u], other, own, ALU.is_equal))
                    dve.tensor_tensor(q4[:, u, 0:8], q4[:, u, 0:8], tie, ALU.mult)
                    link(dve.tensor_tensor(q4[:, u, 8:16, 8:16], q4[:, u, 8:16, 8:16], tie[:, :, 0:8], ALU.mult))
                link(dve.tensor_tensor(cmp_gt, cmp_gt, cmp_eq, ALU.add))
                link(dve.tensor_reduce(rank[:, t0 * E:(t0 + 4) * E].rearrange("p (t e) -> p t e", t=4),
                                       g4, AX.X, ALU.add))
                for f in {8: (0, 1), 12: (2, 3)}.get(t0, ()):
                    leaf_matrix(0, 0, f)
            link(dve.tensor_tensor(ties, ident, onesd[:], ALU.subtract))
            link(dve.tensor_scalar(chosen, rank, float(TOPK), None, ALU.is_lt))
            dve.wait_ge(exp_done, 1)
            link(dve.tensor_tensor(chosen, chosen, exps, ALU.mult))
            link(dve.tensor_reduce(total, by_token(chosen), AX.X, ALU.add))
            link(dve.reciprocal(total, total))
            link(dve.tensor_tensor(by_token(share), by_token(chosen),
                                   total.unsqueeze(2).broadcast_to([P, TT, E]), ALU.mult))
            for x in range(2):
                link(dve.tensor_copy(dense[:, x * PAIRS * TT:(x + 1) * PAIRS * TT].rearrange(
                    "p (e t) -> p t e", e=PAIRS), share.rearrange("p (t e x) -> p t e x", t=TT, x=2)[:, :, :, x]))

        def halves(ap, m, half):
            return ap.rearrange("p (n x m) -> p n x m", x=2, m=m)[:, :, half]

        def blocks(ap, m):
            return ap.rearrange("p (n m) -> p n m", m=m)

        @block.sync
        def _(sp):
            def load_gu(i, src_up, src_gate):
                sp.dma_start(wu[:, i * 2 * P:(i + 1) * 2 * P], src_up).then_inc(wgu_in[i], 16)
                sp.dma_start(wg[:, i * 2 * P:(i + 1) * 2 * P], src_gate).then_inc(wgu_in[i], 16)

            def load_d(i, row):
                lo, hi = (0, 3) if i == 0 else (3, FT)
                sp.dma_start(wd[:, lo * HID:hi * HID], row[:, lo * HID:hi * HID]).then_inc(wd_in[i], 16)

            for i in range(FT):
                cols = slice(i * 2 * P, (i + 1) * 2 * P)
                load_gu(i, wupT[0][:, cols], wgT[0][:, cols])
            for i in range(2):
                load_d(i, wdT[0])
            with sp.Fori(0, PAIRS - 1) as p:
                last = p * NTB + (NTB - 1)

                def row(t):
                    return t[bass.ds(p + 1, 1)].rearrange("o p n -> p (o n)")

                for i in range(FT):
                    sp.wait_ge(ffn_mm.sem, ffn_mm.at(last, i + 1))
                    cols = slice(i * 2 * P, (i + 1) * 2 * P)
                    load_gu(i, row(wupT)[:, cols], row(wgT)[:, cols])
                sp.wait_ge(y_mm.sem, y_mm.at(last, SLOTS - 1))
                load_d(0, row(wdT))
                sp.wait_ge(y_mm.sem, y_mm.at(last + 1, CARRY))
                load_d(1, row(wdT))
            for i in range(FT):
                sp.wait_ge(wgu_in[i], 32 * PAIRS)
            for s in wd_in:
                sp.wait_ge(s, 16 * PAIRS)

        def htile(j):
            return hT[:, j * TB:(j + 1) * TB]

        @block.gpsimd
        def _(pool):
            for s in (prod_ready, decay_ready, span_ready, w_ready, us_ready, wk_ready, pool_step):
                pool.sem_inc(s.sem, s.per)
            pool.memset(decay[:], 1.0)
            pool.memset(kn[:], 0.0).then_inc(cleared, 1)

            def prepare(r, c, turn, first=False):
                k, q = inb[c][:, 0:HT], inb[c][:, HT:2 * HT]
                a = inb[c][:, 3 * HT:4 * HT]
                step = [0]

                def link(ins):
                    step[0] += 1
                    ins.then_inc(pool_step.sem, 1)
                    pool.wait_ge(pool_step.sem, pool_step.at(r, step[0]))

                pool.wait_ge(in_done[c], turn * 16 + 16)
                pool.wait_ge(nb_done[c], turn * 16 + 16)
                kl, bl, al = blocks(k, LEAF), blocks(runs[:], LEAF), blocks(a, LEAF)
                pool.wait_ge(span_ready.sem, span_ready.at(r, 0))
                link(pool.tensor_tensor(runs[:], k, nb[c][:], ALU.mult))

                def products(f):
                    for j in FILLS[f]:
                        n = LEAF - 1 - j
                        ins = pool.tensor_tensor(column(prod[f % 2], j, COL[FILLS[f][0]]),
                                                 bl[:, :, j:j + 1].broadcast_to([P, NM, n]),
                                                 kl[:, :, j + 1:LEAF], ALU.mult)
                    ins.then_inc(prod_ready.sem, 1)

                pool.wait_ge(kq_mm.sem, kq_mm.at(r, 0))
                products(0)
                pool.wait_ge(prep_mm.sem, prep_mm.at(r, 4 - 8))
                products(1)
                pool.wait_ge(prep_used.sem, prep_used.at(r, 4 - 8))
                for j in range(LEAF - 3, -1, -1):
                    n = LEAF - 2 - j
                    ins = pool.tensor_tensor(column(decay, j)[:, :, 1:], column(decay, j + 1),
                                             al[:, :, j + 1:j + 2].broadcast_to([P, NM, n]), ALU.mult)
                    if j:
                        link(ins)
                ins.then_inc(decay_ready.sem, 1)
                pool.wait_ge(prep_mm.sem, prep_mm.at(r, 1))
                products(2)
                pool.wait_ge(prep_mm.sem, prep_mm.at(r, 2))
                products(3)
                if not first:
                    pool.wait_ge(o_ready.sem, o_ready.at(r, -1))
                    pool.wait_ge(z_ready.sem, z_ready.at(r, 2 - 2))
                pool.wait_ge(prod_ready.sem, prod_ready.at(r, 4))
                even, odd = halves(a, 1, 0), halves(a, 1, 1)
                pool.tensor_tensor(blocks(runa[2][:], 1), even, odd, ALU.mult)
                pool.memset(halves(prec[:], 1, 0), 1.0)
                pool.memset(halves(runs[:], 1, 1), 1.0)
                pool.tensor_copy(halves(prec[:], 1, 1), even)
                link(pool.tensor_copy(halves(runs[:], 1, 0), odd))
                m = 2
                while m < CH:
                    nblk = H * CH // m
                    whole = runa[m][:].rearrange("p (n x) -> p n x", x=2)
                    dst = tot[c] if m == CH // 2 else runa[2 * m]
                    pool.tensor_tensor(blocks(dst[:], 1), whole[:, :, 0:1], whole[:, :, 1:2], ALU.mult)
                    pool.tensor_copy(blocks(pre[m][c][:], m), halves(prec[:], m, 1))
                    if m < LEAF:
                        link(pool.tensor_copy(blocks(suf[m][c][:], m), halves(runs[:], m, 0)))
                    else:
                        link(pool.tensor_tensor(blocks(suf[m][c][:], m), halves(runs[:], m, 0),
                                                halves(nb[c][:], m, 0), ALU.mult))
                    pool.tensor_tensor(halves(prec[:], m, 1), halves(prec[:], m, 1),
                                       whole[:, :, 0:1].broadcast_to([P, nblk // 2, m]), ALU.mult)
                    link(pool.tensor_tensor(halves(runs[:], m, 0), halves(runs[:], m, 0),
                                            whole[:, :, 1:2].broadcast_to([P, nblk // 2, m]), ALU.mult))
                    if m == 4:
                        pool.wait_ge(prep_mm.sem, prep_mm.at(r, 3))
                        pool.tensor_tensor(prod[0][:], k, q, ALU.mult).then_inc(prod_ready.sem, 1)
                    m *= 2
                pool.tensor_tensor(sufc[c][:], runs[:], nb[c][:], ALU.mult).then_inc(span_ready.sem, 1)
                assert step[0] == POOL_STEPS

            prepare(0, 0, 0, first=True)
            with pool.Fori(0, PAIRS) as p, pool.Fori(0, NTB) as b:
                n = p * NTB + b
                for c in range(2):
                    m = n * 2 + c
                    prepare(m + 1, 1 - c, n + c)
                    pool.wait_ge(u_ready.sem, u_ready.at(m, 4))
                    pool.tensor_tensor(w[:], z[:], nb[c][:], ALU.mult).then_inc(w_ready.sem, 1)
                    pool.wait_ge(w_ready.sem, w_ready.at(m, 1))
                    pool.tensor_tensor(blocks(us[:, 0:256], 2), halves(w[:], 2, 0), blocks(suf[2][c][:], 2),
                                       ALU.mult)
                    pool.tensor_tensor(blocks(us[:, 256:512], 4), halves(w[:], 4, 0), blocks(suf[4][c][:], 4),
                                       ALU.mult).then_inc(us_ready.sem, 1)
                    pool.wait_ge(uts_mm.sem, uts_mm.at(m, 1))
                    pool.wait_ge(kq_cp.sem, kq_cp.at(m, 1))
                    pool.tensor_tensor(w[:], w[:], kq[c][:], ALU.mult).then_inc(wk_ready.sem, 1)

        @block.tensor
        def _(pe):
            for s in (z_mm, ktr_mm, prep_mm, kq_mm, ut_mm, c_mm, s_mm, st_mm, uts_mm, cs_mm, ffn_mm, y_mm):
                pe.sem_inc(s.sem, s.per)

            def leaf_dots(r, f):
                pe.wait_ge(prod_ready.sem, prod_ready.at(r, f + 1))
                if f >= 2:
                    pe.wait_ge(prep_used.sem, prep_used.at(r, f - 1))
                cols = sum(NM * (LEAF - 1 - j) for j in FILLS[f])
                pe.matmul(leaf_bank[f % 2][:, 0:cols], ones[:], prod[f % 2][:, 0:cols],
                          start=True, stop=True).then_inc(prep_mm.sem, 1)

            def kq_dots(r):
                pe.wait_ge(prod_ready.sem, prod_ready.at(r, 5))
                pe.wait_ge(prep_used.sem, prep_used.at(r, 3))
                pe.matmul(bank_p[:], ones[:], prod[0][:], start=True, stop=True).then_inc(kq_mm.sem, 1)

            def kq3(c):
                return inb[c][:, 0:2 * HT].rearrange("p (x h t) -> p x h t", x=2, h=H)

            def gram8(r, c):
                pe.wait_ge(prep_used.sem, prep_used.at(r, 4))
                pe.wait_ge(kc_cp.sem, kc_cp.at(r, 1))
                for o in range(2):
                    t = o * 16
                    mm = pe.matmul(bank_z[0][:, o * 256:(o + 1) * 256], kc[8][:, o * P:(o + 1) * P],
                                   kq3(c)[:, :, :, t + 8:t + 16], start=True, stop=True)
                mm.then_inc(prep_mm.sem, 1)

            def gram16(r, c):
                pe.wait_ge(kq_cp.sem, kq_cp.at(r, 1))
                for g in range(2):
                    mm = pe.matmul(bank_p[:, g * 256:(g + 1) * 256], kc[16][:, g * P:(g + 1) * P],
                                   kq3(c)[:, :, 8 * g:8 * g + 8, 16:32], start=True, stop=True)
                mm.then_inc(prep_mm.sem, 1)

            def gram_small(r, c, levels, use):
                pe.wait_ge(prep_used.sem, prep_used.at(r, use))
                for i, m in enumerate(levels):
                    for g in range(2):
                        mm = pe.matmul(bank_p[:, (2 * i + g) * P:(2 * i + g + 1) * P],
                                       kc[m][:, g * P:(g + 1) * P] if m > 1 else
                                       inb[c][:, g * 256:(g + 1) * 256].rearrange("p (n x) -> p x n", x=2)[:, 0],
                                       halves(inb[c][:, HT + g * 256:HT + (g + 1) * 256], m, 1),
                                       start=True, stop=True)
                mm.then_inc(prep_mm.sem, 1)

            def experts(p, n, b, slot):
                if slot < FT:
                    pe.wait_ge(wgu_in[slot], p * 32 + 32)
                    pe.wait_ge(h_done.sem, h_done.at(n, slot))
                    if slot % 4 == 0:
                        pe.wait_ge(cs_used.sem, cs_used.at(n * 2 + slot // 4, 0))
                    for bank, wt in ((bank_gate, wg), (bank_up, wu)):
                        for k in range(KT):
                            mm = pe.matmul(bank[:], wt[:, (slot * KT + k) * P:(slot * KT + k + 1) * P],
                                           xn3[:, k, bass.ds(b * TB + HALO, TB)],
                                           start=(k == 0), stop=(k == KT - 1))
                    mm.then_inc(ffn_mm.sem, 1)
                for j in SLOT_OUTPUTS[slot]:
                    output(p, n, j)

            def output(p, n, j):
                second, tok = OUTPUTS[j]
                if j == CARRY:
                    for s in wd_in:
                        pe.wait_ge(s, p * 16 + 16)
                if j < SLOTS - 1:
                    pe.wait_ge(y_used.sem, y_used.at(n, j))
                pe.wait_ge(h_done.sem, h_done.at(n - 1 if j < CARRY else n, FT if second else 4))
                tok *= P
                rows = [(j, 0, P) for j in range(4, FT)] + [(3, FH, P)] if second else \
                    [(j, 0, P) for j in range(3)] + [(3, 0, FH)]
                for i, (t, lo, hi) in enumerate(rows):
                    mm = pe.matmul(output_bank[j][:, 0:HID], htile(t)[lo:hi, tok:tok + P],
                                   wd[lo:hi, t * HID:(t + 1) * HID],
                                   start=(i == 0), stop=(i == len(rows) - 1))
                mm.then_inc(y_mm.sem, 1)

            def level_turn(m, i, src, groups):
                pe.wait_ge(u_ready.sem, u_ready.at(m, i))
                if i > 1:
                    pe.wait_ge(ut_cp.sem, ut_cp.at(m, i - 1))
                for g in range(groups):
                    mm = pe.transpose(bank_t[:, g * P:(g + 1) * P], src[:, g * P:(g + 1) * P], ident)
                mm.then_inc(ut_mm.sem, 1)

            def level_sum(m, i, c, first, groups):
                pe.wait_ge(ut_cp.sem, ut_cp.at(m, i))
                if i == 1:
                    pe.wait_ge(cs_used.sem, cs_used.at(m, 0))
                else:
                    pe.wait_ge(c_used.sem, c_used.at(m, i - 1))
                for g in range(groups):
                    mm = pe.matmul(bank_c[:, g * 256:(g + 1) * 256], ut[:, g * P:(g + 1) * P],
                                   gram[c][:, (first + g) * 256:(first + g + 1) * 256], start=True, stop=True)
                mm.then_inc(c_mm.sem, 1)

            pe.wait_ge(in_done[0], 16)
            pe.wait_ge(wd_in[1], 16)
            for f in range(4):
                leaf_dots(0, f)
            kq_dots(0)
            gram8(0, 0)
            gram16(0, 0)
            gram_small(0, 0, (1, 2), 6)
            gram_small(0, 0, (4,), 7)
            pe.wait_ge(cleared, 2)
            with pe.Fori(0, PAIRS) as p, pe.Fori(0, NTB) as b:
                n = p * NTB + b
                for c in range(2):
                    m = n * 2 + c
                    r, rc = m + 1, 1 - c
                    pe.wait_ge(s_ready.sem, s_ready.at(m, 0))
                    for h in range(H):
                        if h % 8 == 0:
                            pe.wait_ge(st_cp.sem, st_cp.at(m, 0 if h else -2))
                        mm = pe.matmul(bank_z[h // 8][:, (h % 8) * 64:(h % 8 + 1) * 64].rearrange(
                            "p (x t) -> p x t", x=2), stT[:, h * D:(h + 1) * D],
                            kq3(c)[:, :, h, :], start=True, stop=True)
                        if h % 8 == 7:
                            mm.then_inc(z_mm.sem, 1)
                    pe.wait_ge(prep_used.sem, prep_used.at(m, 8))
                    for g in range(4):
                        mm = pe.transpose(bank_p[:, g * P:(g + 1) * P], inb[c][:, g * P:(g + 1) * P], ident)
                    mm.then_inc(ktr_mm.sem, 1)
                    experts(p, n, b, 4 * c)
                    level_turn(m, 1, u8[0], 1)
                    pe.wait_ge(kn_cp.sem, kn_cp.at(m, 4))
                    leaf_dots(r, 0)
                    level_sum(m, 1, c, 0, 1)
                    pe.wait_ge(z_ready.sem, z_ready.at(m, 2))
                    leaf_dots(r, 1)
                    experts(p, n, b, 4 * c + 1)
                    level_turn(m, 2, u16, 2)
                    leaf_dots(r, 2)
                    level_sum(m, 2, c, 2, 2)
                    leaf_dots(r, 3)
                    experts(p, n, b, 4 * c + 2)
                    level_turn(m, 3, u8[1], 1)
                    kq_dots(r)
                    level_sum(m, 3, c, 1, 1)
                    pe.wait_ge(in_done[rc], (n + c) * 16 + 16)
                    gram8(r, rc)
                    experts(p, n, b, 4 * c + 3)
                    gram16(r, rc)
                    level_turn(m, 4, uc, 4)
                    pe.wait_ge(ut_cp.sem, ut_cp.at(m, 4))
                    pe.wait_ge(prep_used.sem, prep_used.at(r, 5))

                    def state_sum(g):
                        pe.matmul(bank_z[g % 2][:], utc[:, g * P:(g + 1) * P], kn[:, g * 512:(g + 1) * 512],
                                  start=True, stop=True).then_inc(s_mm.sem, 1)

                    state_sum(0)
                    state_sum(1)
                    pe.wait_ge(us_ready.sem, us_ready.at(m, 1))
                    pe.wait_ge(h_done.sem, h_done.at(n, FT if c else 4))
                    for g in range(2):
                        pe.transpose(bank_t[:, g * P:(g + 1) * P], w[:, g * 256:(g + 1) * 256].rearrange(
                            "p (n x) -> p x n", x=2)[:, 0], ident)
                    for g in range(2):
                        pe.transpose(bank_t[:, (2 + g) * P:(3 + g) * P], us[:, g * P:(g + 1) * P], ident)
                    for g in range(2):
                        mm = pe.transpose(bank_up[:, g * P:(g + 1) * P], us[:, (2 + g) * P:(3 + g) * P], ident)
                    mm.then_inc(uts_mm.sem, 1)
                    def state_turn(g):
                        pe.wait_ge(s_ready.sem, s_ready.at(m, g + 1))
                        if g < 2:
                            pe.wait_ge(uts_cp.sem, uts_cp.at(m, 1))
                        else:
                            pe.wait_ge(st_cp.sem, st_cp.at(m, g - 1))
                        bank = bank_up if g % 2 else bank_t
                        for x in range(4):
                            mm = pe.transpose(bank[:, x * P:(x + 1) * P],
                                              st[:, (4 * g + x) * D:(4 * g + x + 1) * D], ident)
                        mm.then_inc(st_mm.sem, 1)

                    for g in range(2):
                        pe.wait_ge(s_ready.sem, s_ready.at(m, g + 1))
                        state_sum(2 + g)
                    state_turn(0)
                    state_turn(1)
                    gram_small(r, rc, (1, 2), 6)
                    pe.wait_ge(c_used.sem, c_used.at(m, 3))
                    if c:
                        pe.wait_ge(y_used.sem, y_used.at(n, SLOTS))
                    for g in range(6):
                        dst = bank_c[:, g * P:(g + 1) * P] if g < 4 else bank_gate[:, (g - 4) * P:(g - 3) * P]
                        mm = pe.matmul(dst, uts[:, g * P:(g + 1) * P], grams[c][:, g * P:(g + 1) * P],
                                       start=True, stop=True)
                    mm.then_inc(cs_mm.sem, 1)
                    state_turn(2)
                    state_turn(3)
                    gram_small(r, rc, (4,), 7)
            for j in range(CARRY):
                output(PAIRS, PAIRS * NTB, j)

        @block.scalar
        def _(act):
            for s in (o_out, kn_cp, a_cp, kc_cp, kq_cp, ut_cp, st_cp, uts_cp, silu_done, st_scaled):
                act.sem_inc(s.sem, s.per)

            def copy(dst, src):
                return act.copy(dst, src)

            def load(c, row):
                act.dma_start(inb[c][:], row.rearrange("o p n -> p (o n)")[:, 0:4 * HT]).then_inc(in_done[c], 16)

            def load_beta(c, m):
                act.dma_start(nb[c][:], betas[bass.ds(m, 1)].rearrange("o p n -> p (o n)").broadcast_to([P, HT])
                              ).then_inc(nb_done[c], 16)

            def kq_dots(r, c):
                act.wait_ge(kq_mm.sem, kq_mm.at(r, 1))
                copy(kq[c][:], bank_p[:]).then_inc(kq_cp.sem, 1)

            def experts(n, slot):
                if slot < FT:
                    act.wait_ge(ffn_mm.sem, ffn_mm.at(n, slot + 1))
                    act.wait_ge(y_mm.sem, y_mm.at(n, 0 if slot < 3 else CARRY))
                    act.activation(htile(slot), bank_gate[:], ACT.Silu).then_inc(silu_done.sem, 1)

            def scale_state(m, c, g):
                if g == 0:
                    act.wait_ge(st_mm.sem, st_mm.at(m, 0))
                    act.wait_ge(span_ready.sem, span_ready.at(m, 1))
                for h in range(4 * g, 4 * g + 4):
                    own = st[:, h * D:(h + 1) * D]
                    ins = act.activation(own, own, ACT.Identity, scale=tot[c][:, h:h + 1])
                ins.then_inc(st_scaled.sem, 1)

            def turned(m, i, cols):
                act.wait_ge(ut_mm.sem, ut_mm.at(m, i))
                copy((utc if i == 4 else ut)[:, 0:cols], bank_t[:, 0:cols]).then_inc(ut_cp.sem, 1)

            def store(row):
                act.dma_start(ospill[bass.ds(row, 1)].rearrange("o p n -> p (o n)"), ob[:]
                              ).then_inc(o_out.sem, 16)

            def compact(c, turn):
                act.wait_ge(in_done[c], turn * 16 + 16)
                k = inb[c][:, 0:HT]
                copy(kc[8][:].rearrange("p (o h t) -> p o h t", o=2, h=H),
                     k.rearrange("p (h o x t) -> p x o h t", h=H, o=2, x=2)[:, 0])
                for m in (2, 4, 16):
                    ins = copy(blocks(kc[m][:], m), halves(k, m, 0))
                ins.then_inc(kc_cp.sem, 1)

            for c in range(2):
                load(c, spill[FRONT + c:FRONT + c + 1])
                load_beta(c, c)
            act.wait_ge(shift_done, 1)
            act.activation(exps, shifted, ACT.Exp).then_inc(exp_done, 1)
            compact(0, 0)
            kq_dots(0, 0)
            act.activation(uts[:, 0:1], ident[:, 0:1], ACT.Silu).then_inc(table_in, 1)
            act.wait_ge(table_in, 1)
            act.wait_ge(cleared, 2)
            with act.Fori(0, PAIRS) as p, act.Fori(0, NTB) as b:
                n = p * NTB + b
                for c in range(2):
                    m = n * 2 + c
                    act.wait_ge(ktr_mm.sem, ktr_mm.at(m, 1))
                    for x in range(4):
                        rows = slice(x * CH, (x + 1) * CH)
                        copy(kn4[rows, :, x], bank_p[rows, :].rearrange("p (g d) -> p g d", g=4)
                             ).then_inc(kn_cp.sem, 1)
                    act.wait_ge(o_ready.sem, o_ready.at(m, 0))
                    copy(a_cur[:], inb[c][:, 3 * HT:4 * HT]).then_inc(a_cp.sem, 1)
                    store(m)
                    act.wait_ge(z_ready.sem, z_ready.at(m, 2))
                    act.wait_ge(a_cp.sem, a_cp.at(m, 1))
                    load(c, spill[bass.ds(m + (FRONT + 2), 1)])
                    compact(1 - c, n + c)
                    experts(n, 4 * c)
                    turned(m, 1, P)
                    scale_state(m, c, 0)
                    experts(n, 4 * c + 1)
                    turned(m, 2, 2 * P)
                    scale_state(m, c, 1)
                    experts(n, 4 * c + 2)
                    turned(m, 3, P)
                    kq_dots(m + 1, 1 - c)
                    scale_state(m, c, 2)
                    scale_state(m, c, 3)
                    experts(n, 4 * c + 3)
                    turned(m, 4, 4 * P)
                    act.wait_ge(us_ready.sem, us_ready.at(m, 1))
                    load_beta(c, m + 2)
                    act.wait_ge(uts_mm.sem, uts_mm.at(m, 1))
                    copy(uts[:, 0:4 * P], bank_t[:])
                    copy(uts[:, 4 * P:6 * P], bank_up[:, 0:2 * P]).then_inc(uts_cp.sem, 1)
                    for g in range(4):
                        act.wait_ge(st_mm.sem, st_mm.at(m, g + 1))
                        copy(stT[:, g * 512:(g + 1) * 512], (bank_up if g % 2 else bank_t)[:]
                             ).then_inc(st_cp.sem, 1)
            act.wait_ge(o_ready.sem, o_ready.at(NCH, 0))
            store(NCH)
            act.wait_ge(o_out.sem, o_out.at(0, 16 * (NCH + 1)))
            for c in range(2):
                act.wait_ge(in_done[c], 16 * (NCH // 2 + 1))
                act.wait_ge(nb_done[c], 16 * (NCH // 2 + 1))

        @block.vector
        def _(dve):
            for s in (z_ready, u_ready, prep_used, c_used, s_ready, cs_used, o_ready, dve_step,
                      h_done, y_used):
                dve.sem_inc(s.sem, s.per)
            z3, zq3 = heads(z[:]), heads(zq[:])

            def mul(o, x, y):
                return dve.tensor_tensor(o, x, y, ALU.mult)

            def add(o, x, y):
                return dve.tensor_tensor(o, x, y, ALU.add)

            def leaf_matrix(r, c, f):
                dve.wait_ge(prep_mm.sem, prep_mm.at(r, f + 1))
                if f == 0:
                    dve.wait_ge(decay_ready.sem, decay_ready.at(r, 1))
                cols = slice(COL[FILLS[f][0]], COL[FILLS[f][0]] + sum(NM * (LEAF - 1 - j) for j in FILLS[f]))
                mul(leafm[c][:, cols], leaf_bank[f % 2][:, 0:cols.stop - cols.start], decay[:, cols]
                    ).then_inc(prep_used.sem, 1)

            def masked(r, i, bank, parts):
                dve.wait_ge(prep_mm.sem, prep_mm.at(r, i))
                for dst, col, x, mask in parts:
                    ins = mul(dst.rearrange("p (x n) -> p x n", x=x),
                              bank[:, col:col + x * P].rearrange("p (x n) -> p x n", x=x),
                              mask.unsqueeze(1).broadcast_to([P, x, P]))
                ins.then_inc(prep_used.sem, 1)

            def grams8(r, c):
                masked(r, 5, bank_z[0], [(gram[c][:, 0:512], 0, 4, blk8)])

            def grams16(r, c):
                masked(r, 6, bank_p, [(gram[c][:, 512:1024], 0, 4, blk16)])

            def grams12(r, c):
                masked(r, 7, bank_p, [(grams[c][:, 0:256], 0, 2, ident), (grams[c][:, 256:512], 256, 2, blk2)])

            def grams4(r, c):
                masked(r, 8, bank_p, [(grams[c][:, 512:768], 0, 2, blk4)])

            def output(n, j):
                second, tok = OUTPUTS[j]
                unit = n + (NTB - 1) if j < CARRY else n
                acc = yacc[:, bass.ds((unit % NTB) * (TB // P * HID) + tok * HID, HID)]
                first = (PAIRS * TT if second else 0) - (TB // P if j < CARRY else 0) + tok
                dve.wait_ge(y_mm.sem, y_mm.at(n, j + 1))
                dve.scalar_tensor_tensor(out=acc, in0=output_bank[j][:, 0:HID],
                                         scalar=dense[:, bass.ds(n * (TB // P) + first, 1)], in1=acc,
                                         op0=ALU.mult, op1=ALU.add).then_inc(y_used.sem, 1)

            routing(dve, leaf_matrix)
            grams8(0, 0)
            for t in (ob, stT):
                dve.memset(t[:], 0.0)
            grams16(0, 0)
            dve.memset(hT[:], 0.0)
            grams12(0, 0)
            dve.memset(st[:], 0.0).then_inc(cleared, 1)
            dve.wait_ge(cleared, 2)
            grams4(0, 0)
            with dve.Fori(0, PAIRS) as p, dve.Fori(0, NTB) as b:
                n = p * NTB + b
                for c in range(2):
                    m = n * 2 + c
                    r, rc = m + 1, 1 - c
                    marks = [0]

                    def mark(ins):
                        marks[0] += 1
                        ins.then_inc(dve_step.sem, 1)
                        return marks[0]

                    def need(k):
                        dve.wait_ge(dve_step.sem, dve_step.at(m, k))

                    def link(ins):
                        need(mark(ins))

                    def experts(slot):
                        if slot < FT:
                            dve.wait_ge(silu_done.sem, silu_done.at(n, slot + 1))
                            mul(htile(slot), htile(slot), bank_up[:]).then_inc(h_done.sem, 1)
                        for j in SLOT_OUTPUTS[slot]:
                            output(n, j)

                    def leaf(i):
                        for j in range(LEAF - 1):
                            k, t = LEAF - 1 - j, i * LEAF + j
                            part = tmp[:, 0:H * k].rearrange("p (h d) -> p h d", h=H)
                            link(mul(part, column(leafm[c], j).rearrange("p (h l) t -> p h l t", h=H)[:, :, i],
                                     z3[:, :, t:t + 1].broadcast_to([P, H, k])))
                            link(add(z3[:, :, t + 1:t + 1 + k], z3[:, :, t + 1:t + 1 + k], part))

                    dve.wait_ge(span_ready.sem, span_ready.at(m, 1))
                    v3 = heads(inb[c][:, 2 * HT:3 * HT])
                    p3 = heads(prec[:])
                    for x in range(2):
                        dve.wait_ge(z_mm.sem, z_mm.at(m, x + 1))
                        hs = slice(8 * x, 8 * x + 8)
                        zz = bank_z[x][:].rearrange("p (h x t) -> p h x t", h=8, x=2)
                        k1 = mark(mul(z3[:, hs], zz[:, :, 0], p3[:, hs]))
                        k2 = mark(mul(zq3[:, hs], zz[:, :, 1], p3[:, hs]))
                        need(k1)
                        dve.tensor_tensor(z3[:, hs], z3[:, hs], v3[:, hs], ALU.subtract).then_inc(z_ready.sem, 1)
                    dve.wait_ge(z_ready.sem, z_ready.at(m, 2))

                    def pair_level(i, width, t0):
                        g = width // 8
                        o = (t0 - 8) // 16 if width == 8 else 0
                        dve.wait_ge(c_mm.sem, c_mm.at(m, i))
                        cc = bank_c[:, 0:g * 256].rearrange("p (g x h t) -> p g x h t", g=g, x=2, t=width)
                        span = pre[width][c][:].rearrange("p (g h o t) -> p g h o t", g=g, o=16 // width,
                                                          t=width)[:, :, :, o]
                        zk = z3[:, :, t0:t0 + width].rearrange("p (g h) t -> p g h t", g=g)
                        zqk = zq3[:, :, t0:t0 + width].rearrange("p (g h) t -> p g h t", g=g)
                        tk = tmp[:, 0:H * width].rearrange("p (g h t) -> p g h t", g=g, t=width)
                        tq = tmpq[:, 0:H * width].rearrange("p (g h t) -> p g h t", g=g, t=width)
                        k1 = mark(mul(tk, cc[:, :, 0], span))
                        mul(tq, cc[:, :, 1], span).then_inc(c_used.sem, 1)
                        need(k1)
                        k2 = mark(add(zk, zk, tk))
                        dve.wait_ge(c_used.sem, c_used.at(m, i))
                        mark(add(zqk, zqk, tq))
                        need(k2)

                    dve.wait_ge(prep_used.sem, prep_used.at(m, 4))
                    leaf(0)
                    sp8 = [suf[8][c][:].rearrange("p (h o t) -> p h o t", h=H, o=2)[:, :, o] for o in range(2)]
                    mul(heads(u8[0]), z3[:, :, 0:8], sp8[0]).then_inc(u_ready.sem, 1)
                    experts(4 * c)
                    leaf_matrix(r, rc, 0)
                    pair_level(1, 8, 8)
                    leaf(1)
                    mul(heads(u16), z3[:, :, 0:16], heads(suf[16][c][:])).then_inc(u_ready.sem, 1)
                    experts(4 * c + 1)
                    leaf_matrix(r, rc, 1)
                    leaf_matrix(r, rc, 2)
                    pair_level(2, 16, 16)
                    leaf(2)
                    mul(heads(u8[1]), z3[:, :, 16:24], sp8[1]).then_inc(u_ready.sem, 1)
                    experts(4 * c + 2)
                    leaf_matrix(r, rc, 3)
                    pair_level(3, 8, 24)
                    leaf(3)
                    mul(uc[:], z[:], sufc[c][:]).then_inc(u_ready.sem, 1)
                    grams8(r, rc)
                    grams16(r, rc)
                    experts(4 * c + 3)
                    for g in range(4):
                        dve.wait_ge(s_mm.sem, s_mm.at(m, g + 1))
                        dve.wait_ge(st_scaled.sem, st_scaled.at(m, g + 1))
                        own = st[:, g * 512:(g + 1) * 512]
                        add(own, own, bank_z[g % 2][:]).then_inc(s_ready.sem, 1)
                    grams12(r, rc)
                    dve.wait_ge(cs_mm.sem, cs_mm.at(m, 1))
                    k1 = mark(add(halves(zq[:], 1, 1), halves(zq[:], 1, 1), blocks(bank_c[:, 0:256], 1)))
                    k2 = mark(mul(blocks(tmpq[:, 0:256], 2), blocks(bank_c[:, 256:512], 2),
                                  blocks(pre[2][c][:], 2)))
                    mul(blocks(tmpq[:, 256:512], 4), blocks(bank_gate[:, 0:256], 4), blocks(pre[4][c][:], 4)
                        ).then_inc(cs_used.sem, 1)
                    need(k2)
                    k2 = mark(add(halves(zq[:], 2, 1), halves(zq[:], 2, 1), blocks(tmpq[:, 0:256], 2)))
                    need(k2)
                    link(add(halves(zq[:], 4, 1), halves(zq[:], 4, 1), blocks(tmpq[:, 256:512], 4)))
                    dve.wait_ge(o_out.sem, o_out.at(m, 16))
                    link(mul(ob[:], zq[:], a_cur[:]))
                    dve.wait_ge(wk_ready.sem, wk_ready.at(m, 1))
                    add(ob[:], ob[:], w[:]).then_inc(o_ready.sem, 1)
                    grams4(r, rc)
                    dve.wait_ge(o_ready.sem, o_ready.at(m, 1))
                    assert marks[0] == DVE_STEPS, marks[0]
            for j in range(CARRY):
                output(PAIRS * NTB, j)


def output_phase(nc, ps, spill, ospill, woT, yacc, lns, eps, centre, onesd, out):
    with ExitStack() as ctx:
        def sb(name, n):
            return ctx.enter_context(nc.sbuf_tensor(name, [P, n], F32))

        def counted(name, per, first=None):
            return Counted(ctx.enter_context(nc.semaphore(name)), per, first)

        def two(name, n):
            return [sb(f"{name}{x}", n) for x in range(2)]

        wo = sb("wo", H * HID)
        o = two("o", CPB * HT)
        g = two("g", CPB * HT)
        og = two("og", CPB * HT)
        sq = sb("osq", CPB * HT)
        rs = sb("ors", CPB * HT)
        on = two("on", HT)
        wo_in = ctx.enter_context(nc.semaphore("wo_in"))
        o_in = [ctx.enter_context(nc.semaphore(f"o_in{x}")) for x in range(2)]
        g_in = [ctx.enter_context(nc.semaphore(f"g_in{x}")) for x in range(2)]
        centre_mm = counted("o_centre_mm", CPB)
        squared = counted("o_squared", CPB)
        var_mm = counted("o_var_mm", CPB)
        logged = counted("o_logged", CPB)
        rs_ready = counted("o_rs", CPB)
        normed = counted("o_normed", CPB)
        gated = counted("o_gated", CPB)
        proj_mm = counted("o_proj_mm", 1, 2)
        y_ready = counted("y_ready", 1, 2)
        y_out = ctx.enter_context(nc.semaphore("y_out"))
        block = ctx.enter_context(nc.Block())
        bank_centre, bank_var, bank_proj = ps[0:4], ps[4:6], ps[6:8]

        def part(t, c):
            return t[:, c * HT:(c + 1) * HT]

        def tiles(engine, step):
            step(0, 0)
            with engine.Fori(0, TT // 2 - 2) as n:
                step(n * 2 + 1, 1)
                step(n * 2 + 2, 0)
            step(TT - 3, 1)
            step(TT - 2, 0)
            step(TT - 1, 1)

        @block.sync
        def _(sp):
            def load_o(x, t):
                sp.dma_start(o[x][:].rearrange("p (c n) -> p c n", c=CPB),
                             ospill[bass.ds(t * CPB + 1, CPB)].rearrange("c p n -> p c n")).then_inc(o_in[x], 16)

            def load_g(x, t):
                sp.dma_start(g[x][:].rearrange("p (c n) -> p c n", c=CPB),
                             spill[bass.ds(t * CPB + FRONT, CPB), :, G_ * HT:NT * HT].rearrange("c p n -> p c n")
                             ).then_inc(g_in[x], 16)

            def store(t):
                sp.wait_ge(y_ready.sem, y_ready.at(t, 1))
                sp.dma_start(out[bass.ds(t, 1)].rearrange("o p c -> p (o c)"),
                             yacc[:, bass.ds(t * HID, HID)]).then_inc(y_out, 16)

            def step(t, x):
                if not (isinstance(t, int) and t >= TT - 2):
                    sp.wait_ge(centre_mm.sem, centre_mm.at(t, CPB))
                    load_o(x, t + 2)
                    sp.wait_ge(gated.sem, gated.at(t, CPB))
                    load_g(x, t + 2)
                if not (isinstance(t, int) and t == 0):
                    store(t - 1)

            load_o(0, 0)
            sp.dma_start(wo[:], woT).then_inc(wo_in, 16)
            load_g(0, 0)
            load_o(1, 1)
            load_g(1, 1)
            tiles(sp, step)
            store(TT - 1)
            sp.wait_ge(y_out, 16 * TT)

        @block.tensor
        def _(pe):
            for s in (centre_mm, var_mm, proj_mm):
                pe.sem_inc(s.sem, s.first)

            def centred(t, c, x):
                pe.wait_ge(normed.sem, normed.at(t, c + 1 - CPB))
                pe.matmul(bank_centre[c][:], centre, part(o[x], c), start=True, stop=True
                          ).then_inc(centre_mm.sem, 1)

            def variance(t, c):
                pe.wait_ge(squared.sem, squared.at(t, c + 1))
                pe.wait_ge(logged.sem, logged.at(t, c - 1))
                pe.matmul(bank_var[c % 2][:], onesd[:], part(sq, c), start=True, stop=True
                          ).then_inc(var_mm.sem, 1)

            def project(t, x):
                pe.wait_ge(wo_in, 16)
                pe.wait_ge(gated.sem, gated.at(t, CPB))
                pe.wait_ge(y_ready.sem, y_ready.at(t, -1))
                for h in range(H):
                    mm = pe.matmul(bank_proj[x][:, 0:HID], og[x][:, h * P:(h + 1) * P],
                                   wo[:, h * HID:(h + 1) * HID], start=(h == 0), stop=(h == H - 1))
                mm.then_inc(proj_mm.sem, 1)

            def step(t, x):
                first = isinstance(t, int) and t == 0
                pe.wait_ge(o_in[x], (t - x) * 8 + 16)
                for c in range(CPB):
                    centred(t, c, x)
                    if c:
                        variance(t, c - 1)
                variance(t, CPB - 1)
                if not first:
                    project(t - 1, 1 - x)

            tiles(pe, step)
            project(TT - 1, 1)

        @block.scalar
        def _(act):
            for s in (squared, logged, rs_ready):
                act.sem_inc(s.sem, s.per)

            def square(t, c):
                act.wait_ge(centre_mm.sem, centre_mm.at(t, c + 1))
                act.wait_ge(var_mm.sem, var_mm.at(t, c + 1 - CPB))
                act.activation(part(sq, c), bank_centre[c][:], ACT.Square).then_inc(squared.sem, 1)

            def step(t, x):
                square(t, 0)
                for c in range(CPB):
                    if c + 1 < CPB:
                        square(t, c + 1)
                    act.wait_ge(var_mm.sem, var_mm.at(t, c + 1))
                    act.wait_ge(normed.sem, normed.at(t, c + 1 - CPB))
                    act.activation(part(rs, c), bank_var[c % 2][:], ACT.Ln, bias=eps[:, 0:1]
                                   ).then_inc(logged.sem, 1)
                for c in range(CPB):
                    act.wait_ge(logged.sem, logged.at(t, c + 1))
                    act.activation(part(rs, c), part(rs, c), ACT.Exp, scale=-0.5).then_inc(rs_ready.sem, 1)

            tiles(act, step)

        @block.vector
        def _(dve):
            for s in (normed, gated, y_ready):
                dve.sem_inc(s.sem, s.first)

            def add(t, x):
                dve.wait_ge(proj_mm.sem, proj_mm.at(t, 1))
                acc = yacc[:, bass.ds(t * HID, HID)]
                dve.tensor_tensor(acc, acc, bank_proj[x][:, 0:HID], ALU.add).then_inc(y_ready.sem, 1)

            def step(t, x):
                for c in range(CPB):
                    y = c % 2
                    dve.wait_ge(rs_ready.sem, rs_ready.at(t, c + 1))
                    dve.scalar_tensor_tensor(out=on[y][:], in0=bank_centre[c][:], scalar=lns[:, 0:1],
                                             in1=part(rs, c), op0=ALU.mult, op1=ALU.mult
                                             ).then_inc(normed.sem, 1)
                    if c == 0:
                        dve.wait_ge(g_in[x], (t - x) * 8 + 16)
                        dve.wait_ge(proj_mm.sem, proj_mm.at(t, -1))
                    dve.wait_ge(normed.sem, normed.at(t, c + 1))
                    dve.scalar_tensor_tensor(out=og[x][:].rearrange("p (h c t) -> p c h t", h=H, c=CPB)[:, c],
                                             in0=heads(on[y][:]), scalar=lns[:, 1:2],
                                             in1=heads(part(g[x], c)), op0=ALU.add, op1=ALU.mult
                                             ).then_inc(gated.sem, 1)
                if not (isinstance(t, int) and t == 0):
                    add(t - 1, 1 - x)

            tiles(dve, step)
            add(TT - 1, 1)


_OUT = "y_out_dram"


def kernel(**inputs):
    import numpy as np
    import concourse.bacc as bacc
    from concourse.bass_utils import run_bass_kernel_spmd

    def get(name):
        return np.asarray(inputs["L0_" + name])

    def columns(w):
        n = w.shape[0]
        return w.T.reshape(KT, P, n).transpose(1, 0, 2).reshape(P, KT * n)

    def per_head(v):
        return v.reshape(H, D).T

    def expert_columns(w):
        t = w.reshape(PAIRS, FT, P, KT, P)
        return t.transpose(0, 4, 1, 3, 2).reshape(PAIRS, P, FT * KT * P)

    x = get("attn_x").reshape(S, HID)
    taps = np.stack([get(f"attn_{n}c_w").reshape(H, D, TAPS) for n in "kqv"])
    e = np.arange(P)
    masks = [(e[:, None] // m == e[None, :] // m) for m in (1, 2, 4, 8, 16)]
    ties = np.tile((np.arange(E)[None, :] < np.arange(8)[:, None]).reshape(1, P), (P, 1))
    arrays = {
        "x": x,
        "xT": columns(x),
        "projT": np.stack([columns(get(f"attn_W{n}")) for n in "kqvag"]),
        "wbT": columns(get("attn_Wb")),
        "gateT": columns(get("ffn_gate_inp")),
        "convw": taps.transpose(2, 0, 1, 3).reshape(P, 3 * H * TAPS),
        "chan": np.concatenate([per_head(get(n)) for n in ("attn_kc_b", "attn_qc_b", "attn_vc_b", "attn_ba")], 1),
        "bb": get("attn_bb").reshape(H, 1),
        "lnp": np.stack([get("attn_ln_g"), get("attn_ln_b")], 1),
        "woT": get("attn_Wo").T.reshape(H, D, HID).transpose(1, 0, 2).reshape(D, H * HID),
        "wupT": expert_columns(get("ffn_W_up")),
        "wgT": expert_columns(get("ffn_W_gate")),
        "wdT": get("ffn_W_down").transpose(0, 2, 1).reshape(PAIRS, FT, P, HID).transpose(0, 2, 1, 3)
               .reshape(PAIRS, P, FT * HID),
        "consts": np.concatenate([*masks, ties], 1).astype(np.float32),
    }
    arrays = {n: np.ascontiguousarray(a) for n, a in arrays.items()}
    nc = bacc.Bacc("TRN2", target_bir_lowering=False, num_devices=1)
    args = [nc.dram_tensor(f"{n}_dram", a.shape, F32, kind="ExternalInput").ap() for n, a in arrays.items()]
    out = nc.dram_tensor(_OUT, (TT, P, HID), F32, kind="ExternalOutput").ap()
    build(nc, *args, out)
    r = run_bass_kernel_spmd(nc, [{f"{n}_dram": a for n, a in arrays.items()}], core_ids=[0])
    return r.results[0][_OUT].reshape(1, S, HID)
```
